# Optimizing a Trainium2 kernel written in Bass

```python
import numpy as np
import jax
import jax.numpy as jnp

def _softmax(x, axis=-1):
    return jax.nn.softmax(x, axis=axis)

def _gelu(x):
    return jax.nn.gelu(x, approximate=True)

def _silu(x):
    return jax.nn.silu(x)

def _sigmoid(x):
    return jax.nn.sigmoid(x)

def _layernorm(x, axis=-1, eps=1e-05):
    m = jnp.mean(x, axis=axis, keepdims=True)
    v = jnp.var(x, axis=axis, keepdims=True)
    return (x - m) / jnp.sqrt(v + eps)

def _scatter_add(tgt, idx, src, axis=0):
    return tgt.at[idx].add(src)

def _segment_sum(src, seg, n):
    return jax.ops.segment_sum(src, seg, n)
kernel_name = 'mk_flamingo_gated_d1_seqx_r8_024e00'

def setup_inputs(seed: int=0):
    np.random.seed(seed)
    _w = jnp.asarray

    def _rec_inputs():
        import jax
        import jax.numpy as jnp
        _rk = jax.random.key(seed)
        x = -0.0002928 + 1 * jax.random.normal(jax.random.fold_in(_rk, 1), (32, 56, 128), jnp.float32)
        _lenS = 56 - jax.random.randint(jax.random.fold_in(_rk, 7), (32,), 0, max(1, 56 // 4) + 1, jnp.int32)
        _lenS2 = 1500 - jax.random.randint(jax.random.fold_in(_rk, 8), (32,), 0, max(1, 1500 // 4) + 1, jnp.int32)
        _ctx_1024P = jax.random.normal(jax.random.fold_in(_rk, 11), (32, 16, 128), jnp.float32)
        _ctx_1024c = jax.random.dirichlet(jax.random.fold_in(_rk, 511), 0.3 * jnp.ones((16,), jnp.float32), (32, 1500))
        _ctx_1024t = jnp.einsum('bsk,bkd->bsd', _ctx_1024c, _ctx_1024P)
        _ctx_1024t = _ctx_1024t * jax.lax.rsqrt(jnp.mean(jnp.square(_ctx_1024t)) + 1e-12) * 0.953939
        ctx_1024 = -1.39393e-06 + 0.999914 * (_ctx_1024t + 0.3 * jax.random.normal(jax.random.fold_in(_rk, 611), (32, 1500, 128), jnp.float32))
        _g = jax.random.normal(jax.random.fold_in(_rk, 9001), (2, 1), jnp.float32)
        _g = jnp.sign(_g) * jnp.maximum(jnp.abs(_g), 1.0) + (_g == 0) * 1.0
        g_xattn = _g[0]
        g_ffn = _g[1]
        return (x, ctx_1024, g_xattn, g_ffn)
    x, ctx_1024, g_xattn, g_ffn = _rec_inputs()

    def _L0_xattn_setup():
        import jax, jax.numpy as jnp
        import numpy as np
        B, S, D = (2, 256, 128)
        H, DK, DV = (16, 64, 64)
        NEG = -1000000000.0
        key = jax.random.key(seed)
        ks = jax.random.split(key, 7)
        scale = 1.0 / np.sqrt(D)
        return {'Q': jax.random.normal(ks[0], (B, S, D), dtype=jnp.float32), 'K': jax.random.normal(ks[1], (B, S, D), dtype=jnp.float32), 'V': jax.random.normal(ks[2], (B, S, D), dtype=jnp.float32), 'Wq': jax.random.normal(ks[3], (D, H * DK), dtype=jnp.float32) * scale, 'Wk': jax.random.normal(ks[4], (D, H * DK), dtype=jnp.float32) * scale, 'Wv': jax.random.normal(ks[5], (D, H * DV), dtype=jnp.float32) * scale, 'Wo': jax.random.normal(ks[6], (H * DV, D), dtype=jnp.float32) * scale}
    _L0_xattn_all = _L0_xattn_setup()
    _L0_xattn_in = {k: v for k, v in _L0_xattn_all.items() if k in ('Wq', 'Wk', 'Wv', 'Wo')}
    del _L0_xattn_all

    def _L0_ffn_setup():
        import jax, jax.numpy as jnp
        import numpy as np
        D = 128
        H = 16
        HD = D // H
        L = 64
        E = 8
        B, T = (4, 256)
        EPS = 1e-06

        def _glorot(k, shape):
            fan_in, fan_out = (shape[-2], shape[-1])
            lim = np.sqrt(6.0 / (fan_in + fan_out)).astype(np.float32)
            return jax.random.uniform(k, shape, jnp.float32, -lim, lim)

        def _rmsnorm(x, gamma):
            return gamma * x * jax.lax.rsqrt(jnp.mean(x * x, axis=-1, keepdims=True) + EPS)
        key = jax.random.key(seed)
        ks = jax.random.split(key, 8)
        return {'x': jax.random.normal(ks[0], (B, T, D), jnp.float32), 'gamma1': jnp.ones((D,), jnp.float32), 'Wq': _glorot(ks[1], (D, D)), 'bq': jnp.zeros((D,), jnp.float32), 'Wdown': _glorot(ks[2], (D, L)), 'bdown': jnp.zeros((L,), jnp.float32), 'Wup': _glorot(ks[3], (L, 2 * D)), 'bup': jnp.zeros((2 * D,), jnp.float32), 'Wo': _glorot(ks[4], (D, D)), 'bo': jnp.zeros((D,), jnp.float32), 'gamma2': jnp.ones((D,), jnp.float32), 'Wg': _glorot(ks[5], (D, E)), 'bg': jnp.zeros((E,), jnp.float32), 'We': _glorot(ks[6], (E, D, D))}
    _L0_ffn_all = _L0_ffn_setup()
    _L0_ffn_in = {k: v for k, v in _L0_ffn_all.items() if k in ('gamma1', 'Wq', 'bq', 'Wdown', 'bdown', 'Wup', 'bup', 'Wo', 'bo', 'gamma2', 'Wg', 'bg', 'We')}
    del _L0_ffn_all
    return {'x': x, 'ctx_1024': ctx_1024, 'g_xattn': g_xattn, 'g_ffn': g_ffn, 'L0_xattn_Wq': _L0_xattn_in['Wq'], 'L0_xattn_Wk': _L0_xattn_in['Wk'], 'L0_xattn_Wv': _L0_xattn_in['Wv'], 'L0_xattn_Wo': _L0_xattn_in['Wo'], 'L0_ffn_gamma1': _L0_ffn_in['gamma1'], 'L0_ffn_Wq': _L0_ffn_in['Wq'], 'L0_ffn_bq': _L0_ffn_in['bq'], 'L0_ffn_Wdown': _L0_ffn_in['Wdown'], 'L0_ffn_bdown': _L0_ffn_in['bdown'], 'L0_ffn_Wup': _L0_ffn_in['Wup'], 'L0_ffn_bup': _L0_ffn_in['bup'], 'L0_ffn_Wo': _L0_ffn_in['Wo'], 'L0_ffn_bo': _L0_ffn_in['bo'], 'L0_ffn_gamma2': _L0_ffn_in['gamma2'], 'L0_ffn_Wg': _L0_ffn_in['Wg'], 'L0_ffn_bg': _L0_ffn_in['bg'], 'L0_ffn_We': _L0_ffn_in['We']}

def reference(x, ctx_1024, g_xattn, g_ffn, L0_xattn_Wq, L0_xattn_Wk, L0_xattn_Wv, L0_xattn_Wo, L0_ffn_gamma1, L0_ffn_Wq, L0_ffn_bq, L0_ffn_Wdown, L0_ffn_bdown, L0_ffn_Wup, L0_ffn_bup, L0_ffn_Wo, L0_ffn_bo, L0_ffn_gamma2, L0_ffn_Wg, L0_ffn_bg, L0_ffn_We):
    import jax
    import jax.numpy as jnp

    def _L0_xattn_ref(Q, K, V, Wq, Wk, Wv, Wo):
        import jax, jax.numpy as jnp
        import numpy as np
        B, S, D = (2, 256, 128)
        H, DK, DV = (16, 64, 64)
        NEG = -1000000000.0
        b, sq, _ = Q.shape
        sk = K.shape[1]
        q = (Q @ Wq).reshape(b, sq, H, DK).transpose(0, 2, 1, 3)
        k = (K @ Wk).reshape(b, sk, H, DK).transpose(0, 2, 1, 3)
        v = (V @ Wv).reshape(b, sk, H, DV).transpose(0, 2, 1, 3)
        scores = jnp.einsum('bhqd,bhkd->bhqk', q, k) / jnp.sqrt(jnp.float32(DK))
        causal = jnp.tril(jnp.ones((sq, sk), dtype=bool))
        scores = jnp.where(causal[None, None], scores, NEG)
        attn = jax.nn.softmax(scores, axis=-1)
        out = jnp.einsum('bhqk,bhkd->bhqd', attn, v)
        out = out.transpose(0, 2, 1, 3).reshape(b, sq, H * DV)
        return out @ Wo

    def _L0_ffn_ref(x, gamma1, Wq, bq, Wdown, bdown, Wup, bup, Wo, bo, gamma2, Wg, bg, We):
        import jax, jax.numpy as jnp
        import numpy as np
        D = 128
        H = 16
        HD = D // H
        L = 64
        E = 8
        B, T = (4, 256)
        EPS = 1e-06

        def _glorot(k, shape):
            fan_in, fan_out = (shape[-2], shape[-1])
            lim = np.sqrt(6.0 / (fan_in + fan_out)).astype(np.float32)
            return jax.random.uniform(k, shape, jnp.float32, -lim, lim)

        def _rmsnorm(x, gamma):
            return gamma * x * jax.lax.rsqrt(jnp.mean(x * x, axis=-1, keepdims=True) + EPS)
        b, t = (x.shape[0], x.shape[1])
        h = _rmsnorm(x, gamma1)
        q = (h @ Wq + bq).reshape(b, t, H, HD)
        kv = ((h @ Wdown + bdown) @ Wup + bup).reshape(b, t, H, 2 * HD)
        k, v = jnp.split(kv, 2, axis=-1)
        att = jnp.einsum('bthd,btgd->bthg', q, k) / np.sqrt(HD).astype(np.float32)
        att = jax.nn.softmax(att, axis=-1)
        out = jnp.einsum('bthg,btgd->bthd', att, v).reshape(b, t, D)
        x = x + (out @ Wo + bo)
        h2 = _rmsnorm(x, gamma2)
        gate = jax.nn.softmax(h2 @ Wg + bg, axis=-1)
        combined = jnp.einsum('btd,edf,bte->btf', h2, We, gate)
        return x + combined
    x = x + jnp.tanh(g_xattn[0]) * _L0_xattn_ref(_layernorm(x, axis=-1), ctx_1024, ctx_1024, L0_xattn_Wq, L0_xattn_Wk, L0_xattn_Wv, L0_xattn_Wo)
    x = x + jnp.tanh(g_ffn[0]) * _L0_ffn_ref(_layernorm(x, axis=-1), L0_ffn_gamma1, L0_ffn_Wq, L0_ffn_bq, L0_ffn_Wdown, L0_ffn_bdown, L0_ffn_Wup, L0_ffn_bup, L0_ffn_Wo, L0_ffn_bo, L0_ffn_gamma2, L0_ffn_Wg, L0_ffn_bg, L0_ffn_We)
    return x

_drawn_inputs = setup_inputs


def setup_inputs(seed=0):
    import zlib

    import numpy as np

    out = dict(_drawn_inputs(seed))
    spreads = {'L0_ffn_gamma1': (1.0, 0.2),
     'L0_ffn_bq': (0.0, 0.352),
     'L0_ffn_bdown': (0.0, 0.285),
     'L0_ffn_bup': (0.0, 0.1),
     'L0_ffn_bo': (0.0, 0.1),
     'L0_ffn_gamma2': (1.0, 0.2),
     'L0_ffn_bg': (0.0, 0.349)}
    factors = {}
    for name, (base, spread) in spreads.items():
        noise = np.random.default_rng([zlib.crc32(name.encode()), seed]).standard_normal(out[name].shape)
        drawn = base * np.exp(spread * noise) if base else spread * noise
        out[name] = jnp.asarray(drawn.astype(out[name].dtype))
    for name, factor in factors.items():
        out[name] = (out[name] * factor).astype(out[name].dtype)
    return out
```

```python
from contextlib import ExitStack

import numpy as np

import concourse.bass as bass
from concourse import mybir

ALU = mybir.AluOpType
ACT = mybir.ActivationFunctionType
AX = mybir.AxisListType
F32 = mybir.dt.float32
BF16 = mybir.dt.bfloat16

HP = 8
HIDE = -1e30
LN_EPS = 1e-5
RMS_EPS = 1e-6


def build(nc, x, ctx_kv, g_xattn, g_ffn, wq, wk, wv, wo, gamma1, fwq, fbq, fwdown, fbdown, fwup, fbup,
          fwo, fbo, gamma2, fwg, fbg, fwe, out):
    B, S, D = x.shape
    DK = 64
    H = wq.shape[1] // DK
    C = H // 2
    NP = B // 2
    T = 2 * S
    G = 64
    TG = G + S
    L = fwdown.shape[1]
    FH = 16
    FD = D // FH
    E = fwg.shape[1]
    HC = C // 2
    assert D == 128 and H * DK == C * 128 and fwup.shape[1] == 2 * D and T <= 128

    x_pairs = x.rearrange("(n b) s d -> n (b s) d", b=2)
    out_pairs = out.rearrange("(n b) s d -> n (b s) d", b=2)
    ctx_pairs = ctx_kv.rearrange("(n b) s d -> n b s d", b=2)

    with ExitStack() as stack:
        def sb(name, shape, dt=F32):
            return stack.enter_context(nc.sbuf_tensor(name, shape, dt))

        def two(name, shape, dt=F32):
            return [sb(f"{name}_{i}", shape, dt) for i in range(2)]

        def sem(name):
            return stack.enter_context(nc.semaphore(name))

        ps_qv = stack.enter_context(nc.psum_tensor("ps_qv", [128, 2, 512], F32))
        ps_ko = stack.enter_context(nc.psum_tensor("ps_ko", [128, 2, 512], F32))
        ps_se = stack.enter_context(nc.psum_tensor("ps_se", [128, 2, 512], F32))
        ps_x = stack.enter_context(nc.psum_tensor("ps_x", [128, 512], F32))
        ps_kv = stack.enter_context(nc.psum_tensor("ps_kv", [128, 512], F32))

        ident = sb("ident", [128, 128])
        ident_b = sb("ident_b", [128, 128], BF16)
        hide = sb("hide", [128, S])
        hide_b = sb("hide_b", [128, C, S], BF16)
        minus_half = sb("minus_half", [128, 2])
        wq_sb = sb("wq_sb", [128, C, 128])
        wk_sb = sb("wk_sb", [128, C, 128])
        wv_sb = sb("wv_sb", [128, 2, C, DK])
        wo_sb = sb("wo_sb", [128, C, D])
        gam = sb("gam", [128, 2])
        fwq_sb = sb("fwq_sb", [128, D])
        fwdown_sb = sb("fwdown_sb", [128, L])
        fbdown_sb = sb("fbdown_sb", [128, 1])
        fwup_in = sb("fwup_in", [128, 2 * D])
        fwup_sb = sb("fwup_sb", [128, 2, D])
        fwo_sb = sb("fwo_sb", [128, D])
        fwg_sb = sb("fwg_sb", [128, E])
        fwe_sb = sb("fwe_sb", [128, E, D])
        fbq_sb = sb("fbq_sb", [128, D])
        fbo_sb = sb("fbo_sb", [128, D])
        fbg_sb = sb("fbg_sb", [128, E])
        gates_in = sb("gates_in", [128, 2])
        gates = sb("gates", [128, 2])

        x_sb = two("x_sb", [128, D])
        xres = two("xres", [128, D])
        ctx_sb = two("ctx_sb", [128, D])
        st1 = two("st1", [128, 6])
        mv1 = two("mv1", [128, 2])
        ve1 = two("ve1", [128, 1])
        rstd1 = two("rstd1", [128, 1])
        xln = two("xln", [128, D])
        xcT = two("xcT", [128, 2, 120])
        qT = two("qT", [128, C, T])
        kT = two("kT", [128, C, T])
        v_sb = two("v_sb", [128, 2, C, DK])
        nmax = two("nmax", [128, 2, C], BF16)
        probs = two("probs", [128, C, 2, G])
        psums = two("psums", [128, C, 2])
        prinv = two("prinv", [128, C, 2])
        probsT = two("probsT", [128, C, T])
        attnT = two("attnT", [128, C, T])
        x1 = two("x1", [128, D])
        st2 = two("st2", [128, 6])
        mv2 = two("mv2", [128, 2])
        ve2 = two("ve2", [128, 2])
        rstd2 = two("rstd2", [128, 2])
        u_sb = two("u_sb", [128, D])
        h_sb = two("h_sb", [128, D])
        ub_sb = two("ub_sb", [128, D])
        hT = two("hT", [128, T])
        cT = two("cT", [128, T])
        fq = two("fq", [128, D])
        fkv = two("fkv", [128, 2, D])
        prod1 = sb("prod1", [128, FH, FH, FD])
        prod2 = sb("prod2", [128, FH, FD, FH])
        logit = two("logit", [128, FH, FH])
        lmax = two("lmax", [128, FH])
        lshift = two("lshift", [128, FH, FH])
        esum = two("esum", [128, FH])
        einv = two("einv", [128, FH])
        oraw = two("oraw", [128, FH, FD])
        onorm = two("onorm", [128, D])
        oT = two("oT", [128, T])
        x2 = two("x2", [128, D])
        x2sq = sb("x2sq", [128, D])
        ssq = two("ssq", [128, 1])
        ms = two("ms", [128, 1])
        r2 = two("r2", [128, 1])
        r2g = two("r2g", [128, 1])
        x2T = two("x2T", [128, T])
        glog = two("glog", [128, E])
        gmax = two("gmax", [128, 1])
        gexp = two("gexp", [128, E])
        gsum = two("gsum", [128, 1])
        ginv = two("ginv", [128, 1])
        gate = two("gate", [128, E])
        base = two("base", [128, D])
        expert = two("expert", [128, E, D])
        out_sb = two("out_sb", [128, D])

        w_att = sem("w_att")
        w_ffn = sem("w_ffn")
        consts0 = sem("consts0")
        consts = sem("consts")
        scaled = sem("scaled")
        gates_ready = sem("gates_ready")
        names = """xln_ready stats1 moments1 var1 rstd1_ready xc_turned xcT_ready
            q_lo q_hi qT_ready k_lo k_hi kT_ready v_made v_ready scores_made nmax_ready scores_shifted
            probs_exp psum_ready prinv_ready probs_ready p_lo p_hi probsT_ready a_made attnT_ready y_made
            x1_ready stats2 moments2 var2a var2b rstd2_ready u_ready h_ready ub_ready h_turned hT_ready
            fq_made fq_ready c_made cT_ready kv_made kv_ready prod1_pool prod1_ready logit_ready lmax_ready
            lshift_ready e_ready esum_ready einv_ready prod2_ready oraw_ready onorm_ready o_turned oT_ready
            o_made x2_ready ssq_ready ms_ready r2_ready r2g_ready x2_turned x2T_ready glog_made glog_ready gmax_ready
            gexp_ready ginv_ready gate_ready experts_made base_ready experts_ready sum4 sum2 sum1 out_ready stored"""
        x_loaded = [sem(f"x_loaded_{i}") for i in range(2)]
        ctx_loaded = [sem(f"ctx_loaded_{i}") for i in range(2)]
        xres_loaded = [sem(f"xres_loaded_{i}") for i in range(2)]
        s = {n: sem(n) for n in names.split()}

        block = stack.enter_context(nc.Block())

        def run(eng, step):
            for i in range(-4, 0):
                step(i // 2, i % 2)
            rounds = (NP - 4) // 2
            with eng.Fori(0, rounds) as j:
                step(j, 0)
                step(j, 1)
            for i in range(2 * rounds, NP):
                step(i // 2, i % 2)

        def live(i, ahead):
            return not isinstance(i, int) or 0 <= i + ahead < NP

        def counts(eng, i):
            n = (i + 5, i + 4, i + 3, i + 2, i + 1)
            if not isinstance(i, int):
                for v in n:
                    eng.to_reg(v)
            return n

        def wait_alone(eng, name, value):
            eng.wait_ge(consts, 1)
            eng.wait_ge(s[name], value)

        @block.sync
        def _(sp):
            def load(t, p):
                if isinstance(t, int) and not 0 <= t < NP:
                    return
                if not isinstance(t, int) or t >= 2:
                    sp.wait_ge(s["xln_ready"], t - 1)
                sp.dma_start(x_sb[p][0:T, :], x_pairs[t]).then_inc(x_loaded[p], 16)
                if not isinstance(t, int) or t >= 2:
                    sp.wait_ge(s["xc_turned"], t - 1)
                for b in range(2):
                    sp.dma_start(ctx_sb[p][b * S:(b + 1) * S, :], ctx_pairs[t, b, 0:S, :]).then_inc(ctx_loaded[p], 16)

            def load_residual(t, p):
                if isinstance(t, int) and not 0 <= t < NP:
                    return
                if not isinstance(t, int) or t >= 2:
                    sp.wait_ge(s["x1_ready"], t - 1)
                sp.dma_start(xres[p][0:T, :], x_pairs[t]).then_inc(xres_loaded[p], 16)

            def store(t, p):
                if isinstance(t, int) and not 0 <= t < NP:
                    return
                sp.wait_ge(s["out_ready"], t + 1)
                sp.dma_start(out_pairs[t], out_sb[p][0:T, :]).then_inc(s["stored"], 16)

            load(0, 0)
            sp.dma_start(wk_sb[:, :, :], wk.rearrange("d (c f) -> d c f", c=C)).then_inc(w_att, 16)
            load(1, 1)
            sp.dma_start(gam[:, 0:1], gamma1.rearrange("(d o) -> d o", o=1)).then_inc(w_ffn, 16)
            sp.dma_start(gam[:, 1:2], gamma2.rearrange("(d o) -> d o", o=1)).then_inc(w_ffn, 16)
            sp.dma_start(gates_in[:, 0:1], g_xattn.partition_broadcast(128)).then_inc(w_ffn, 16)
            sp.dma_start(gates_in[:, 1:2], g_ffn.partition_broadcast(128)).then_inc(w_ffn, 16)
            sp.dma_start(wo_sb[:, :, :], wo.rearrange("(c p) f -> p c f", c=C)).then_inc(w_att, 16)
            load_residual(0, 0)
            load(2, 0)
            sp.dma_start(fwq_sb[:, :], fwq).then_inc(w_ffn, 16)
            sp.dma_start(fwdown_sb[:, :], fwdown).then_inc(w_ffn, 16)
            sp.dma_start(fbdown_sb[0:L, :], fbdown.rearrange("(d o) -> d o", o=1)).then_inc(w_ffn, 16)
            sp.dma_start(fwup_in[0:L, :], fwup).then_inc(w_ffn, 16)
            sp.dma_start(fwup_in[L:L + 1, :], fbup.rearrange("(o d) -> o d", o=1)).then_inc(w_ffn, 16)
            sp.dma_start(fbq_sb[:, :], fbq.partition_broadcast(128)).then_inc(w_ffn, 16)
            sp.dma_start(fbo_sb[:, :], fbo.partition_broadcast(128)).then_inc(w_ffn, 16)
            sp.dma_start(fbg_sb[:, :], fbg.partition_broadcast(128)).then_inc(w_ffn, 16)
            sp.dma_start(fwo_sb[:, :], fwo).then_inc(w_ffn, 16)
            sp.dma_start(fwg_sb[:, :], fwg).then_inc(w_ffn, 16)
            sp.dma_start(fwe_sb[:, :, :], fwe.rearrange("e d f -> d e f")).then_inc(w_ffn, 16)

            def step(j, p):
                i = 2 * j + p
                load(i + 6, p)
                load_residual(i + 4, p)
                store(i, p)

            for i in range(-3, 0):
                step(i // 2, i % 2)
            rounds = (NP - 6) // 2
            with sp.Fori(0, rounds) as j:
                step(j, 0)
                step(j, 1)
            for i in range(2 * rounds, NP):
                step(i // 2, i % 2)
            sp.wait_ge(s["stored"], 16 * (NP + 1))
        N_FFN_LOADS = 15

        @block.gpsimd
        def _(pool):
            nc.gpsimd.memset(ident[:, :], 0.0)
            nc.gpsimd.memset(hide[:, :], 0.0)
            nc.gpsimd.memset(minus_half[:, :], -0.5)
            for p in range(2):
                nc.gpsimd.memset(probs[p][:, :, :, :], 0.0)
                nc.gpsimd.memset(xcT[p][:, :, :], 0.0).then_inc(consts0, 1)
            pool.wait_ge(consts0, 2)
            nc.gpsimd.affine_select(out=ident[:, :], in_=ident[:, :], compare_op=ALU.not_equal, fill=1.0,
                                    base=0, pattern=[[-1, 128]], channel_multiplier=1).then_inc(consts0, 1)
            pool.wait_ge(consts0, 3)
            for b in range(2):
                h = hide[b * G:(b + 1) * G, :]
                nc.gpsimd.affine_select(out=h, in_=h, compare_op=ALU.is_ge, fill=HIDE, base=0,
                                        pattern=[[-1, S]], channel_multiplier=1).then_inc(consts0, 1)
                pool.wait_ge(consts0, 4 + b)
            nc.gpsimd.tensor_copy(ident_b[:, :], ident[:, :])
            nc.gpsimd.tensor_copy(hide_b[:, :, :], hide[:, :].unsqueeze(1).to_broadcast([128, C, S])).then_inc(consts, 1)

            def step(j, p):
                i, q = 2 * j + p, 1 - p
                nz, na, nb, nc_, nd = counts(pool, i)
                if live(i, 1):
                    pool.wait_ge(s["kv_ready"], nc_)
                    pool.wait_ge(s["fq_ready"], nc_)
                    nc.gpsimd.tensor_tensor(
                        prod1[0:T, 0:HP, :, :],
                        fkv[q][0:T, 0, :].rearrange("p (g d) -> p g d", g=FH).unsqueeze(1).to_broadcast([T, HP, FH, FD]),
                        fq[q][0:T, 0:HP * FD].rearrange("p (h d) -> p h d", h=HP).unsqueeze(2).to_broadcast([T, HP, FH, FD]),
                        ALU.mult).then_inc(s["prod1_pool"], 1)
                if live(i, 4):
                    wait_alone(pool, "moments1", nz)
                    nc.gpsimd.tensor_scalar(ve1[p][0:T, :], mv1[p][0:T, 1:2], LN_EPS, 1.0, ALU.add, ALU.mult).then_inc(s["var1"], 1)
                    pool.wait_ge(s["var1"], nz)
                    nc.gpsimd.tensor_tensor(rstd1[p][0:T, :], ve1[p][0:T, :], minus_half[0:T, 0:1], ALU.pow).then_inc(s["rstd1_ready"], 1)
                if live(i, 0):
                    wait_alone(pool, "ssq_ready", nd)
                    nc.gpsimd.tensor_scalar(ms[p][0:T, :], ssq[p][0:T, :], 1.0 / D, RMS_EPS, ALU.mult, ALU.add).then_inc(s["ms_ready"], 1)
                    pool.wait_ge(s["ms_ready"], nd)
                    nc.gpsimd.tensor_tensor(r2[p][0:T, :], ms[p][0:T, :], minus_half[0:T, 0:1], ALU.pow).then_inc(s["r2_ready"], 1)
                    wait_alone(pool, "r2_ready", nd)
                    nc.gpsimd.tensor_scalar(r2g[p][0:T, :], r2[p][0:T, :], gates[0:T, 1:2], 1.0, ALU.mult, ALU.mult).then_inc(s["r2g_ready"], 1)
                    wait_alone(pool, "ginv_ready", nd)
                    pool.wait_ge(s["r2g_ready"], nd)
                    nc.gpsimd.tensor_scalar(gate[p][0:T, :], gexp[p][0:T, :], ginv[p][0:T, :], r2g[p][0:T, :], ALU.mult, ALU.mult).then_inc(s["gate_ready"], 1)
                if live(i, 2):
                    wait_alone(pool, "moments2", nb)
                    nc.gpsimd.tensor_scalar(ve2[p][0:T, 0:1], mv2[p][0:T, 1:2], LN_EPS, 1.0, ALU.add, ALU.mult).then_inc(s["var2a"], 1)
                    wait_alone(pool, "var2a", nb)
                    nc.gpsimd.tensor_scalar(ve2[p][0:T, 1:2], ve2[p][0:T, 0:1], RMS_EPS, mv2[p][0:T, 1:2], ALU.mult, ALU.add).then_inc(s["var2b"], 1)
                    pool.wait_ge(s["var2b"], nb)
                    nc.gpsimd.tensor_tensor(rstd2[p][0:T, :], ve2[p][0:T, :], minus_half[0:T, :], ALU.pow).then_inc(s["rstd2_ready"], 1)
                    wait_alone(pool, "rstd2_ready", nb)
                    nc.gpsimd.tensor_scalar(u_sb[p][0:T, :], x1[p][0:T, :], mv2[p][0:T, 0:1], rstd2[p][0:T, 0:1],
                                            ALU.subtract, ALU.mult).then_inc(s["u_ready"], 1)
                    pool.wait_ge(s["u_ready"], nb)
                    nc.gpsimd.tensor_tensor(ub_sb[p][0:T, :], u_sb[p][0:T, :], fbo_sb[0:T, :], ALU.add).then_inc(s["ub_ready"], 1)
                if live(i, 0):
                    pool.wait_ge(s["experts_ready"], nd)
                    x = expert[p]
                    nc.gpsimd.tensor_tensor(x[0:T, 0:4, :], x[0:T, 0:4, :], x[0:T, 4:8, :], ALU.add).then_inc(s["sum4"], 1)
                    pool.wait_ge(s["sum4"], nd)
                    nc.gpsimd.tensor_tensor(x[0:T, 0:2, :], x[0:T, 0:2, :], x[0:T, 2:4, :], ALU.add).then_inc(s["sum2"], 1)
                    pool.wait_ge(s["sum2"], nd)
                    nc.gpsimd.tensor_tensor(x[0:T, 0, :], x[0:T, 0, :], x[0:T, 1, :], ALU.add).then_inc(s["sum1"], 1)
                    pool.wait_ge(s["sum1"], nd)
                    pool.wait_ge(s["base_ready"], nd)
                    pool.wait_ge(s["stored"], 16 * nd)
                    nc.gpsimd.tensor_tensor(out_sb[p][0:T, :], x[0:T, 0, :], base[p][0:T, :], ALU.add).then_inc(s["out_ready"], 1)
                if live(i, 3):
                    pool.wait_ge(s["prinv_ready"], na)
                    nc.gpsimd.tensor_tensor(probs[q][0:TG, :, :, 0:S], probs[q][0:TG, :, :, 0:S],
                                            prinv[q][0:TG, :, :].unsqueeze(3).to_broadcast([TG, C, 2, S]),
                                            ALU.mult).then_inc(s["probs_ready"], 1)

            run(pool, step)

        @block.scalar
        def _(act):
            act.dma_start(wq_sb[:, :, :], wq.rearrange("d (c f) -> d c f", c=C)).then_inc(w_att, 16)
            for r in range(2):
                act.dma_start(wv_sb[:, r, :, :], wv.rearrange("d (c r e) -> d r c e", c=C, r=2)[:, r, :, :]).then_inc(w_att, 16)
            act.wait_ge(w_ffn, 16 * N_FFN_LOADS)
            nc.scalar.activation(gates[:, :], gates_in[:, :], ACT.Tanh).then_inc(gates_ready, 1)
            act.wait_ge(consts, 1)

            def chunks(dst, src, done, n, width, ready):
                for half in range(2):
                    if half < len(done):
                        act.wait_ge(s[done[half]], n)
                    last = nc.scalar.copy(dst[:, half * HC:(half + 1) * HC, :],
                                          src[:, half, 0:HC * width].rearrange("p (c s) -> p c s", c=HC))
                last.then_inc(s[ready], 1)

            def step(j, p):
                i, q = 2 * j + p, 1 - p
                nz, na, nb, nc_, nd = counts(act, i)
                if live(i, 3):
                    chunks(qT[q], ps_qv, ("q_lo", "q_hi"), na, T, "qT_ready")
                if live(i, 1):
                    act.wait_ge(s["c_made"], nc_)
                    nc.scalar.activation(cT[q][0:L, :], ps_kv[0:L, 0:T], ACT.Identity, bias=fbdown_sb[0:L, :]).then_inc(s["cT_ready"], 1)
                if live(i, 3):
                    chunks(kT[q], ps_ko, ("k_lo", "k_hi"), na, T, "kT_ready")
                if live(i, 1):
                    act.wait_ge(s["kv_made"], nc_)
                    nc.scalar.copy(fkv[q][0:T, :, :], ps_kv[0:T, 0:2 * D].rearrange("p (n f) -> p n f", n=2)).then_inc(s["kv_ready"], 1)
                if live(i, 0):
                    act.wait_ge(s["o_turned"], nd)
                    nc.scalar.copy(oT[p][:, :], ps_x[:, 0:T]).then_inc(s["oT_ready"], 1)
                if live(i, 3):
                    act.wait_ge(s["v_made"], na)
                    nc.scalar.copy(v_sb[q][:, :, :, :].rearrange("p b c e -> p b (c e)"), ps_qv[:, :, :]).then_inc(s["v_ready"], 1)
                if live(i, 0):
                    act.wait_ge(s["x2_ready"], nd)
                    nc.scalar.activation(x2sq[0:T, :], x2[p][0:T, :], ACT.Square, accum_out=ssq[p][0:T, :]).then_inc(s["ssq_ready"], 1)
                    act.wait_ge(s["x2_turned"], nd)
                    nc.scalar.copy(x2T[p][:, :], ps_x[:, 0:T]).then_inc(s["x2T_ready"], 1)
                if live(i, 2):
                    for half, done in enumerate(("p_lo", "p_hi")):
                        act.wait_ge(s[done], nb)
                        last = nc.scalar.copy(
                            probsT[p][:, half * HC:(half + 1) * HC, :].rearrange("p c (b s) -> p c b s", b=2),
                            ps_qv[:, half, :].rearrange("p (c b s) -> p c b s", c=HC, b=2)[:, :, :, 0:S])
                    last.then_inc(s["probsT_ready"], 1)
                if live(i, 0):
                    act.wait_ge(s["gmax_ready"], nd)
                    nc.scalar.activation(gexp[p][0:T, :], glog[p][0:T, :], ACT.Exp, bias=gmax[p][0:T, :],
                                         accum_out=gsum[p][0:T, :]).then_inc(s["gexp_ready"], 1)
                if live(i, 1):
                    act.wait_ge(s["lshift_ready"], nc_)
                    nc.scalar.activation(ps_kv[0:T, 2 * D:4 * D], lshift[q][0:T, :, :].rearrange("p h g -> p (h g)"), ACT.Exp,
                                         scale=float(FD) ** -0.5).then_inc(s["e_ready"], 1)
                if live(i, 2):
                    chunks(attnT[p], ps_ko, ("a_made",), nb, T, "attnT_ready")
                if live(i, 3):
                    act.wait_ge(s["scores_shifted"], na)
                    nc.scalar.activation(probs[q][0:TG, :, :, 0:S].rearrange("p c r k -> p r c k"),
                                         ps_se[0:TG, :, 0:C * S].rearrange("p r (c k) -> p r c k", c=C), ACT.Exp,
                                         scale=float(DK) ** -0.5).then_inc(s["probs_exp"], 1)
                if live(i, 4):
                    act.wait_ge(s["xc_turned"], nz)
                    nc.scalar.copy(xcT[p][:, :, 0:T], ps_x[:, 0:256].rearrange("p (n s) -> p n s", n=2)[:, :, 0:T]).then_inc(s["xcT_ready"], 1)
                if live(i, 0):
                    act.wait_ge(s["experts_made"], nd)
                    act.wait_ge(s["gate_ready"], nd)
                    for e in range(E):
                        last = nc.scalar.activation(expert[p][0:T, e, :], ps_se[0:T, e // 4, (e % 4) * D:(e % 4 + 1) * D],
                                                    ACT.Copy, scale=gate[p][0:T, e:e + 1])
                    last.then_inc(s["experts_ready"], 1)
                if live(i, 2):
                    act.wait_ge(s["h_turned"], nb)
                    nc.scalar.copy(hT[p][:, :], ps_x[:, 0:T]).then_inc(s["hT_ready"], 1)

            run(act, step)

        @block.vector
        def _(dve):
            for p in range(2):
                ins = nc.vector.memset(cT[p][L:L + 1, :], 1.0)
            ins.then_inc(s["stored"], 16)

            def scale_weights():
                dve.wait_ge(w_ffn, 16 * N_FFN_LOADS)
                nc.vector.tensor_scalar(fwq_sb[:, :], fwq_sb[:, :], gam[:, 0:1], None, ALU.mult)
                nc.vector.tensor_scalar(fwdown_sb[:, :], fwdown_sb[:, :], gam[:, 0:1], None, ALU.mult)
                nc.vector.tensor_scalar(fwg_sb[:, :], fwg_sb[:, :], gam[:, 1:2], None, ALU.mult)
                nc.vector.tensor_scalar(fwe_sb[:, :, :], fwe_sb[:, :, :], gam[:, 1:2], None, ALU.mult)
                up = fwup_in[0:L + 1, :].rearrange("p (h n d) -> p h n d", h=FH, n=2)
                nc.vector.tensor_copy(fwup_sb[0:L + 1, 0, :].rearrange("p (h d) -> p h d", h=FH), up[:, :, 0, :])
                nc.vector.tensor_copy(fwup_sb[0:L + 1, 1, :].rearrange("p (d h) -> p h d", h=FH), up[:, :, 1, :]).then_inc(scaled, 1)
                dve.wait_ge(gates_ready, 1)

            def step(j, p):
                i, q = 2 * j + p, 1 - p
                nz, na, nb, nc_, nd = counts(dve, i)
                if i is not None and isinstance(i, int) and i == -3:
                    scale_weights()
                if live(i, 0):
                    wait_prod2 = s["prod2_ready"]
                    dve.wait_ge(wait_prod2, nd)
                    nc.vector.tensor_reduce(oraw[p][0:T, :, :], prod2[0:T, :, :, :], AX.X, ALU.add).then_inc(s["oraw_ready"], 1)
                    dve.wait_ge(s["oraw_ready"], nd)
                    dve.wait_ge(s["einv_ready"], nd)
                    nc.vector.tensor_tensor(onorm[p][0:T, :].rearrange("p (h d) -> p h d", h=FH), oraw[p][0:T, :, :],
                                            einv[p][0:T, :].unsqueeze(2).to_broadcast([T, FH, FD]), ALU.mult).then_inc(s["onorm_ready"], 1)
                if live(i, 1):
                    dve.wait_ge(s["fq_made"], nc_)
                    nc.vector.tensor_tensor(fq[q][0:T, :], ps_x[0:T, 0:D], fbq_sb[0:T, :], ALU.add).then_inc(s["fq_ready"], 1)
                if live(i, 4):
                    dve.wait_ge(x_loaded[p], 16 * (j + 3))
                    nc.vector.bn_stats(st1[p][0:T, :], x_sb[p][0:T, :]).then_inc(s["stats1"], 1)
                    wait_alone(dve, "stats1", nz)
                    nc.vector.bn_aggr(mv1[p][0:T, :], st1[p][0:T, :]).then_inc(s["moments1"], 1)
                if live(i, 1):
                    dve.wait_ge(s["kv_ready"], nc_)
                    dve.wait_ge(s["fq_ready"], nc_)
                    nc.vector.tensor_tensor(
                        prod1[0:T, HP:FH, :, :],
                        ps_kv[0:T, 0:D].rearrange("p (g d) -> p g d", g=FH).unsqueeze(1).to_broadcast([T, FH - HP, FH, FD]),
                        fq[q][0:T, HP * FD:D].rearrange("p (h d) -> p h d", h=FH - HP).unsqueeze(2).to_broadcast([T, FH - HP, FH, FD]),
                        ALU.mult).then_inc(s["prod1_ready"], 1)
                if live(i, 0):
                    dve.wait_ge(s["o_made"], nd)
                    dve.wait_ge(s["ub_ready"], nd)
                    nc.vector.tensor_tensor(x2[p][0:T, :], ps_x[0:T, 0:D], ub_sb[p][0:T, :], ALU.add).then_inc(s["x2_ready"], 1)
                if live(i, 4):
                    dve.wait_ge(s["rstd1_ready"], nz)
                    nc.vector.tensor_scalar(xln[p][0:T, :], x_sb[p][0:T, :], mv1[p][0:T, 0:1], rstd1[p][0:T, :],
                                            ALU.subtract, ALU.mult).then_inc(s["xln_ready"], 1)
                if live(i, 1):
                    dve.wait_ge(s["prod1_pool"], nc_)
                    dve.wait_ge(s["prod1_ready"], nc_)
                    nc.vector.tensor_reduce(logit[q][0:T, :, :], prod1[0:T, :, :, :], AX.X, ALU.add).then_inc(s["logit_ready"], 1)
                if live(i, 0):
                    dve.wait_ge(s["x2_ready"], nd)
                    nc.vector.scalar_tensor_tensor(out=base[p][0:T, :], in0=x2[p][0:T, :], scalar=gates[0:T, 1:2],
                                                   in1=x1[p][0:T, :], op0=ALU.mult, op1=ALU.add).then_inc(s["base_ready"], 1)
                if live(i, 1):
                    dve.wait_ge(s["logit_ready"], nc_)
                    nc.vector.tensor_reduce(lmax[q][0:T, :], logit[q][0:T, :, :], AX.X, ALU.max).then_inc(s["lmax_ready"], 1)
                    dve.wait_ge(s["lmax_ready"], nc_)
                    nc.vector.tensor_tensor(lshift[q][0:T, :, :], logit[q][0:T, :, :],
                                            lmax[q][0:T, :].unsqueeze(2).to_broadcast([T, FH, FH]),
                                            ALU.subtract).then_inc(s["lshift_ready"], 1)
                if live(i, 3):
                    dve.wait_ge(s["scores_made"], na)
                    nc.vector.tensor_reduce(nmax[q][0:TG, :, :], ps_se[0:TG, :, 0:C * S].rearrange("p r (c k) -> p r c k", c=C),
                                            AX.X, ALU.max, negate=True).then_inc(s["nmax_ready"], 1)
                if live(i, 0):
                    dve.wait_ge(s["glog_made"], nd)
                    dve.wait_ge(s["r2_ready"], nd)
                    nc.vector.scalar_tensor_tensor(out=glog[p][0:T, :], in0=ps_x[0:T, 256:256 + E], scalar=r2[p][0:T, :],
                                                   in1=fbg_sb[0:T, :], op0=ALU.mult, op1=ALU.add).then_inc(s["glog_ready"], 1)
                    dve.wait_ge(s["glog_ready"], nd)
                    nc.vector.tensor_reduce(gmax[p][0:T, :], glog[p][0:T, :], AX.X, ALU.max, negate=True).then_inc(s["gmax_ready"], 1)
                if live(i, 1):
                    dve.wait_ge(s["e_ready"], nc_)
                    nc.vector.tensor_reduce(esum[q][0:T, :], ps_kv[0:T, 2 * D:4 * D].rearrange("p (h g) -> p h g", h=FH),
                                            AX.X, ALU.add).then_inc(s["esum_ready"], 1)
                    nc.vector.tensor_tensor(
                        prod2[0:T, :, :, :],
                        ps_kv[0:T, 2 * D:4 * D].rearrange("p (h g) -> p h g", h=FH).unsqueeze(2).to_broadcast([T, FH, FD, FH]),
                        fkv[q][0:T, 1, :].rearrange("p (d g) -> p d g", d=FD).unsqueeze(1).to_broadcast([T, FH, FD, FH]),
                        ALU.mult).then_inc(s["prod2_ready"], 1)
                    dve.wait_ge(s["esum_ready"], nc_)
                    nc.vector.reciprocal(einv[q][0:T, :], esum[q][0:T, :]).then_inc(s["einv_ready"], 1)
                if live(i, 0):
                    dve.wait_ge(s["gexp_ready"], nd)
                    nc.vector.reciprocal(ginv[p][0:T, :], gsum[p][0:T, :]).then_inc(s["ginv_ready"], 1)
                if live(i, 2):
                    dve.wait_ge(s["y_made"], nb)
                    dve.wait_ge(xres_loaded[p], 16 * (j + 2))
                    nc.vector.scalar_tensor_tensor(out=x1[p][0:T, :], in0=ps_x[0:T, 0:D], scalar=gates[0:T, 0:1],
                                                   in1=xres[p][0:T, :], op0=ALU.mult, op1=ALU.add).then_inc(s["x1_ready"], 1)
                    dve.wait_ge(s["x1_ready"], nb)
                    nc.vector.bn_stats(st2[p][0:T, :], x1[p][0:T, :]).then_inc(s["stats2"], 1)
                    wait_alone(dve, "stats2", nb)
                    nc.vector.bn_aggr(mv2[p][0:T, :], st2[p][0:T, :]).then_inc(s["moments2"], 1)
                if live(i, 3):
                    dve.wait_ge(s["probs_exp"], na)
                    nc.vector.tensor_reduce(psums[q][0:TG, :, :], probs[q][0:TG, :, :, 0:S], AX.X, ALU.add).then_inc(s["psum_ready"], 1)
                    dve.wait_ge(s["psum_ready"], na)
                    nc.vector.reciprocal(prinv[q][0:TG, :, :], psums[q][0:TG, :, :]).then_inc(s["prinv_ready"], 1)
                if live(i, 2):
                    dve.wait_ge(s["rstd2_ready"], nb)
                    nc.vector.tensor_scalar(h_sb[p][0:T, :], x1[p][0:T, :], mv2[p][0:T, 0:1], rstd2[p][0:T, 1:2],
                                            ALU.subtract, ALU.mult).then_inc(s["h_ready"], 1)

            run(dve, step)

        @block.tensor
        def _(pe):
            pe.wait_ge(consts, 1)

            def mm(o, lhsT, rhs, start=True, stop=True):
                return nc.tensor.matmul(o, lhsT, rhs, start=start, stop=stop, skip_group_check=True)

            def project(dst, w, rhs, done):
                for ch in range(C):
                    ins = mm(dst[:, ch // HC, ch % HC * T:(ch % HC + 1) * T], w[:, ch, :], rhs)
                    if ch % HC == HC - 1:
                        ins.then_inc(s[done[ch // HC]], 1)

            def step(j, p):
                i, q = 2 * j + p, 1 - p
                nz, na, nb, nc_, nd = counts(pe, i)
                if isinstance(i, int) and i == -3:
                    pe.wait_ge(w_att, 16 * 5)
                if isinstance(i, int) and i == -1:
                    pe.wait_ge(scaled, 1)
                if live(i, 3):
                    pe.wait_ge(s["xcT_ready"], na)
                    if live(i, 1):
                        pe.wait_ge(s["probsT_ready"], nc_)
                    project(ps_qv, wq_sb, xcT[q][:, 0, 0:T], ("q_lo", "q_hi"))
                if live(i, 1):
                    pe.wait_ge(s["hT_ready"], nc_)
                    mm(ps_x[0:T, 0:D], hT[q][:, :], fwq_sb[:, :]).then_inc(s["fq_made"], 1)
                    if live(i, 0):
                        pe.wait_ge(s["prod2_ready"], nd)
                    mm(ps_kv[0:L, 0:T], fwdown_sb[:, :], hT[q][:, :]).then_inc(s["c_made"], 1)
                if live(i, 3):
                    if live(i, 1):
                        pe.wait_ge(s["attnT_ready"], nc_)
                    project(ps_ko, wk_sb, xcT[q][:, 1, 0:T], ("k_lo", "k_hi"))
                if live(i, 1):
                    pe.wait_ge(s["cT_ready"], nc_)
                    mm(ps_kv[0:T, 0:2 * D], cT[q][0:L + 1, :], fwup_sb[0:L + 1, :, :].rearrange("p n f -> p (n f)")).then_inc(s["kv_made"], 1)
                if live(i, 0):
                    pe.wait_ge(s["onorm_ready"], nd)
                    if live(i, 1):
                        pe.wait_ge(s["fq_ready"], nc_)
                    else:
                        pe.wait_ge(s["glog_ready"], nd - 1)
                    nc.tensor.transpose(ps_x[:, 0:T], onorm[p][0:T, :], ident[0:T, 0:T]).then_inc(s["o_turned"], 1)
                if live(i, 3):
                    pe.wait_ge(s["qT_ready"], na)
                    for bt in range(2):
                        for r in range(2):
                            ins = mm(ps_qv[r * G:(r + 1) * G, bt, :], xcT[q][:, 1, bt * S:bt * S + G],
                                     wv_sb[:, r, :, :].rearrange("p c e -> p (c e)"))
                    ins.then_inc(s["v_made"], 1)
                if live(i, 0):
                    pe.wait_ge(s["oT_ready"], nd)
                    mm(ps_x[0:T, 0:D], oT[p][:, :], fwo_sb[:, :]).then_inc(s["o_made"], 1)
                if live(i, 3):
                    for r in range(2):
                        mm(ps_se[0:TG, r, 0:C * S], ident_b[0:TG, 0:TG], hide_b[0:TG, :, :].rearrange("p c k -> p (c k)"), stop=False)
                    wait_alone(pe, "kT_ready", na)
                    for ch in range(C):
                        for r in range(2):
                            for bt in range(2):
                                ins = mm(ps_se[bt * G:bt * G + S, r, ch * S:(ch + 1) * S],
                                         qT[q][r * G:(r + 1) * G, ch, bt * S:(bt + 1) * S],
                                         kT[q][r * G:(r + 1) * G, ch, bt * S:(bt + 1) * S], start=False, stop=False)
                    ins.then_inc(s["scores_made"], 1)
                if live(i, 0):
                    pe.wait_ge(s["x2_ready"], nd)
                    nc.tensor.transpose(ps_x[:, 0:T], x2[p][0:T, :], ident[0:T, 0:T]).then_inc(s["x2_turned"], 1)
                if live(i, 2):
                    pe.wait_ge(s["probs_ready"], nb)
                    if live(i, 3):
                        pe.wait_ge(s["v_ready"], na)
                    for ch in range(C):
                        ins = nc.tensor.transpose(ps_qv[:, ch // HC, ch % HC * 128:ch % HC * 128 + TG],
                                                  probs[p][0:TG, ch, :, :].rearrange("p r k -> p (r k)"), ident[0:TG, 0:TG])
                        if ch % HC == HC - 1:
                            ins.then_inc(s["p_hi" if ch // HC else "p_lo"], 1)
                if live(i, 0):
                    pe.wait_ge(s["x2T_ready"], nd)
                    mm(ps_x[0:T, 256:256 + E], x2T[p][:, :], fwg_sb[:, :]).then_inc(s["glog_made"], 1)
                if live(i, 2):
                    wait_alone(pe, "probsT_ready", nb)
                    for k in range(C):
                        for r in range(2):
                            ch = (k + r * HC) % C
                            for bt in range(2):
                                ins = mm(ps_ko[r * G:r * G + DK, ch // HC, ch % HC * T + bt * S:ch % HC * T + (bt + 1) * S],
                                         v_sb[p][r * G:r * G + S, bt, ch, :], probsT[p][r * G:r * G + S, ch, bt * S:(bt + 1) * S])
                    ins.then_inc(s["a_made"], 1)
                if live(i, 3):
                    pe.wait_ge(s["nmax_ready"], na)
                    for r in range(2):
                        ins = mm(ps_se[0:TG, r, 0:C * S], ident_b[0:TG, 0:TG],
                                 nmax[q][0:TG, r, :].unsqueeze(2).to_broadcast([TG, C, S]), start=False)
                    ins.then_inc(s["scores_shifted"], 1)
                if live(i, 2):
                    pe.wait_ge(s["attnT_ready"], nb)
                    if live(i, 0):
                        pe.wait_ge(s["glog_ready"], nd)
                    elif live(i, 1):
                        pe.wait_ge(s["fq_ready"], nc_)
                    for ch in range(C):
                        ins = mm(ps_x[0:T, 0:D], attnT[p][:, ch, :], wo_sb[:, ch, :], start=(ch == 0), stop=(ch == C - 1))
                    ins.then_inc(s["y_made"], 1)
                if live(i, 0):
                    if live(i, 3):
                        pe.wait_ge(s["probs_exp"], na)
                    else:
                        pe.wait_ge(s["experts_ready"], nd - 1)
                    for n in range(2):
                        ins = mm(ps_se[0:T, n, :], x2T[p][:, :], fwe_sb[:, n * 4:(n + 1) * 4, :].rearrange("p e f -> p (e f)"))
                    ins.then_inc(s["experts_made"], 1)
                if live(i, 4):
                    pe.wait_ge(s["xln_ready"], nz)
                    pe.wait_ge(ctx_loaded[p], 32 * (j + 3))
                    if live(i, 2):
                        pe.wait_ge(s["x1_ready"], nb)
                    elif live(i, 3) and i > -4:
                        pe.wait_ge(s["xcT_ready"], nz - 1)
                    nc.tensor.transpose(ps_x[:, 0:T], xln[p][0:T, :], ident[0:T, 0:T])
                    nc.tensor.transpose(ps_x[:, 128:128 + T], ctx_sb[p][0:T, :], ident[0:T, 0:T]).then_inc(s["xc_turned"], 1)
                if live(i, 2):
                    pe.wait_ge(s["h_ready"], nb)
                    if live(i, 4):
                        pe.wait_ge(s["xcT_ready"], nz)
                    nc.tensor.transpose(ps_x[:, 0:T], h_sb[p][0:T, :], ident[0:T, 0:T]).then_inc(s["h_turned"], 1)

            run(pe, step)


_INS = ["x", "ctx_1024", "g_xattn", "g_ffn", "L0_xattn_Wq", "L0_xattn_Wk", "L0_xattn_Wv", "L0_xattn_Wo",
        "L0_ffn_gamma1", "L0_ffn_Wq", "L0_ffn_bq", "L0_ffn_Wdown", "L0_ffn_bdown", "L0_ffn_Wup", "L0_ffn_bup",
        "L0_ffn_Wo", "L0_ffn_bo", "L0_ffn_gamma2", "L0_ffn_Wg", "L0_ffn_bg", "L0_ffn_We"]


def kernel(**inputs):
    import concourse.bacc as bacc
    from concourse.bass_utils import run_bass_kernel_spmd

    nc = bacc.Bacc("TRN2", target_bir_lowering=False, num_devices=1)
    arrays, args = {}, []
    for name in _INS:
        a = np.ascontiguousarray(inputs[name])
        arrays[f"in_{name}"] = a
        args.append(nc.dram_tensor(f"in_{name}", a.shape, mybir.dt.from_np(a.dtype), kind="ExternalInput").ap())
    out = nc.dram_tensor("out", inputs["x"].shape, F32, kind="ExternalOutput").ap()
    build(nc, *args, out)
    r = run_bass_kernel_spmd(nc, [arrays], core_ids=[0])
    return r.results[0]["out"]
```

```python
from contextlib import ExitStack

import numpy as np

import concourse.bass as bass
from concourse import mybir

ALU = mybir.AluOpType
ACT = mybir.ActivationFunctionType
AX = mybir.AxisListType
F32 = mybir.dt.float32
BF16 = mybir.dt.bfloat16

HP = 5
WARM_UP = 10
HIDE = -1e30
LN_EPS = 1e-5
RMS_EPS = 1e-6


def build(nc, x, ctx_kv, g_xattn, g_ffn, wq, wk, wv, wo, gamma1, fwq, fbq, fwdown, fbdown, fwup, fbup,
          fwo, fbo, gamma2, fwg, fbg, fwe, out):
    B, S, D = x.shape
    DK = 64
    H = wq.shape[1] // DK
    C = H // 2
    NP = B // 2
    T = 2 * S
    G = 64
    TG = G + S
    L = fwdown.shape[1]
    FH = 16
    FD = D // FH
    E = fwg.shape[1]
    HC = C // 2
    assert D == 128 and H * DK == C * 128 and fwup.shape[1] == 2 * D and T <= 128

    x_pairs = x.rearrange("(n b) s d -> n (b s) d", b=2)
    out_pairs = out.rearrange("(n b) s d -> n (b s) d", b=2)
    ctx_pairs = ctx_kv.rearrange("(n b) s d -> n b s d", b=2)

    with ExitStack() as stack:
        def sb(name, shape, dt=F32):
            return stack.enter_context(nc.sbuf_tensor(name, shape, dt))

        def two(name, shape, dt=F32):
            return [sb(f"{name}_{i}", shape, dt) for i in range(2)]

        def sem(name):
            return stack.enter_context(nc.semaphore(name))

        ps_qkv = stack.enter_context(nc.psum_tensor("ps_qkv", [128, 2, 512], F32))
        ps_pa = stack.enter_context(nc.psum_tensor("ps_pa", [128, 2, 512], F32))
        ps_se = stack.enter_context(nc.psum_tensor("ps_se", [128, 2, 512], F32))
        ps_x = stack.enter_context(nc.psum_tensor("ps_x", [128, 512], F32))
        ps_kv = stack.enter_context(nc.psum_tensor("ps_kv", [128, 512], F32))

        ident = sb("ident", [128, 128])
        ident_b = sb("ident_b", [128, 128], BF16)
        hide = sb("hide", [128, S])
        hide_b = sb("hide_b", [128, C, S], BF16)
        minus_half = sb("minus_half", [128, 2])
        wq_sb = sb("wq_sb", [128, C, 128])
        wk_sb = sb("wk_sb", [128, C, 128])
        wv_sb = sb("wv_sb", [128, 2, C, DK])
        wo_sb = sb("wo_sb", [128, C, D])
        gam = sb("gam", [128, 2])
        fwq_sb = sb("fwq_sb", [128, D])
        fwdown_sb = sb("fwdown_sb", [128, L])
        fbdown_sb = sb("fbdown_sb", [128, 1])
        fwup_in = sb("fwup_in", [128, 2 * D])
        fwup_sb = sb("fwup_sb", [128, 2, D])
        fwo_sb = sb("fwo_sb", [128, D])
        fwg_sb = sb("fwg_sb", [128, E])
        fwe_sb = sb("fwe_sb", [128, E, D])
        fbq_sb = sb("fbq_sb", [128, D])
        fbo_sb = sb("fbo_sb", [128, D])
        fbg_sb = sb("fbg_sb", [128, E])
        gates_in = sb("gates_in", [128, 2])
        gates = sb("gates", [128, 2])

        x_sb = two("x_sb", [128, D])
        xres = two("xres", [128, D])
        ctx_sb = two("ctx_sb", [128, D])
        st1 = two("st1", [128, 6])
        mv1 = two("mv1", [128, 2])
        ve1 = two("ve1", [128, 1])
        rstd1 = two("rstd1", [128, 1])
        xln = two("xln", [128, D])
        xcT = two("xcT", [128, 2, 120])
        qT = two("qT", [128, C, T])
        kT = two("kT", [128, C, T])
        v_sb = two("v_sb", [128, 2, C, DK])
        nmax = two("nmax", [128, 2, C], BF16)
        probs = two("probs", [128, C, 2, G])
        psums = two("psums", [128, C, 2])
        prinv = two("prinv", [128, C, 2])
        probsT = two("probsT", [128, C, T])
        attnT = two("attnT", [128, C, T])
        x1 = two("x1", [128, D])
        st2 = two("st2", [128, 6])
        mv2 = two("mv2", [128, 2])
        ve2 = two("ve2", [128, 2])
        rstd2 = two("rstd2", [128, 2])
        u_sb = two("u_sb", [128, D])
        h_sb = two("h_sb", [128, D])
        ub_sb = two("ub_sb", [128, D])
        hT = two("hT", [128, T])
        cT = two("cT", [128, T])
        fq = two("fq", [128, D])
        fkv = two("fkv", [128, 2, D])
        prod1 = sb("prod1", [128, FH, FH, FD])
        prod2 = sb("prod2", [128, FH, FD, FH])
        logit = two("logit", [128, FH, FH])
        lmax = two("lmax", [128, FH])
        lshift = two("lshift", [128, FH, FH])
        esum = two("esum", [128, FH])
        einv = two("einv", [128, FH])
        oraw = two("oraw", [128, FH, FD])
        onorm = two("onorm", [128, D])
        oT = two("oT", [128, T])
        x2 = two("x2", [128, D])
        x2sq = sb("x2sq", [128, D])
        ssq = two("ssq", [128, 1])
        ms = two("ms", [128, 1])
        r2 = two("r2", [128, 1])
        r2g = two("r2g", [128, 1])
        x2T = two("x2T", [128, T])
        glog = two("glog", [128, E])
        gmax = two("gmax", [128, 1])
        gexp = two("gexp", [128, E])
        gsum = two("gsum", [128, 1])
        ginv = two("ginv", [128, 1])
        gate = two("gate", [128, E])
        base = two("base", [128, D])
        expert = two("expert", [128, E, D])
        out_sb = two("out_sb", [128, D])

        wq_loaded = sem("wq_loaded")
        wk_loaded = sem("wk_loaded")
        wv_loaded = sem("wv_loaded")
        wo_loaded = sem("wo_loaded")
        w_ffn = sem("w_ffn")
        consts0 = sem("consts0")
        consts = sem("consts")
        pads_zeroed = sem("pads_zeroed")
        scaled = sem("scaled")
        gates_ready = sem("gates_ready")
        names = """xln_ready stats1 moments1 var1 rstd1_ready xc_turned xcT_ready
            q_lo q_hi qT_ready k_lo k_hi kT_ready v_made v_ready scores_made nmax_ready scores_shifted
            probs_exp psum_ready prinv_ready probs_ready p_lo p_hi probsT_ready a_made attnT_ready y_made
            x1_ready stats2 moments2 var2a var2b rstd2_ready u_ready h_ready ub_ready h_turned hT_ready
            fq_made fq_ready c_made cT_ready kv_made kv_ready prod1_pool prod1_ready logit_ready lmax_ready
            lshift_ready e_ready esum_ready einv_ready prod2_ready oraw_ready onorm_ready o_turned oT_ready
            o_made x2_ready ssq_ready ms_ready r2_ready r2g_ready x2_turned x2T_ready glog_made glog_ready gmax_ready
            gexp_ready ginv_ready gate_ready experts_made base_ready experts_ready sum4 sum2 sum1 out_ready stored"""
        x_loaded = [sem(f"x_loaded_{i}") for i in range(2)]
        ctx_loaded = [sem(f"ctx_loaded_{i}") for i in range(2)]
        xres_loaded = [sem(f"xres_loaded_{i}") for i in range(2)]
        s = {n: sem(n) for n in names.split()}

        block = stack.enter_context(nc.Block())

        def run(eng, step):
            for i in range(-4, 2):
                step(i // 2, i % 2)
            rounds = (NP - 4) // 2
            with eng.Fori(1, rounds) as j:
                step(j, 0)
                step(j, 1)
            for i in range(2 * rounds, NP):
                step(i // 2, i % 2)

        def live(i, ahead):
            return not isinstance(i, int) or 0 <= i + ahead < NP

        def counts(eng, i):
            n = (i + 5, i + 4, i + 3, i + 2, i + 1)
            if not isinstance(i, int):
                for v in n:
                    eng.to_reg(v)
            return n

        def wait_alone(eng, name, value):
            eng.wait_ge(consts0, 1)
            eng.wait_ge(s[name], value)

        @block.sync
        def _(sp):
            def load(t, p):
                if isinstance(t, int) and not 0 <= t < NP:
                    return
                if not isinstance(t, int) or t >= 2:
                    sp.wait_ge(s["xln_ready"], t - 1)
                sp.dma_start(x_sb[p][0:T, :], x_pairs[t]).then_inc(x_loaded[p], 16)
                if not isinstance(t, int) or t >= 2:
                    sp.wait_ge(s["xc_turned"], t - 1)
                for b in range(2):
                    sp.dma_start(ctx_sb[p][b * S:(b + 1) * S, :], ctx_pairs[t, b, 0:S, :]).then_inc(ctx_loaded[p], 16)

            def load_residual(t, p):
                if isinstance(t, int) and not 0 <= t < NP:
                    return
                if not isinstance(t, int) or t >= 2:
                    sp.wait_ge(s["x1_ready"], t - 1)
                sp.dma_start(xres[p][0:T, :], x_pairs[t]).then_inc(xres_loaded[p], 16)

            def store(t, p):
                if isinstance(t, int) and not 0 <= t < NP:
                    return
                sp.wait_ge(s["out_ready"], t + 1)
                sp.dma_start(out_pairs[t], out_sb[p][0:T, :]).then_inc(s["stored"], 16)

            load(0, 0)
            for r in range(2):
                sp.dma_start(wv_sb[:, r, :, :], wv.rearrange("d (c r e) -> d r c e", c=C, r=2)[:, r, :, :]).then_inc(wv_loaded, 16)
            load(1, 1)
            sp.dma_start(gam[:, 0:1], gamma1.rearrange("(d o) -> d o", o=1)).then_inc(w_ffn, 16)
            sp.dma_start(gam[:, 1:2], gamma2.rearrange("(d o) -> d o", o=1)).then_inc(w_ffn, 16)
            sp.dma_start(gates_in[:, 0:1], g_xattn.partition_broadcast(128)).then_inc(w_ffn, 16)
            sp.dma_start(gates_in[:, 1:2], g_ffn.partition_broadcast(128)).then_inc(w_ffn, 16)
            sp.dma_start(wo_sb[:, :, :], wo.rearrange("(c p) f -> p c f", c=C)).then_inc(wo_loaded, 16)
            load_residual(0, 0)
            load(2, 0)
            sp.dma_start(fwq_sb[:, :], fwq).then_inc(w_ffn, 16)
            sp.dma_start(fwdown_sb[:, :], fwdown).then_inc(w_ffn, 16)
            sp.dma_start(fbdown_sb[0:L, :], fbdown.rearrange("(d o) -> d o", o=1)).then_inc(w_ffn, 16)
            sp.dma_start(fwup_in[0:L, :], fwup).then_inc(w_ffn, 16)
            sp.dma_start(fwup_in[L:L + 1, :], fbup.rearrange("(o d) -> o d", o=1)).then_inc(w_ffn, 16)
            sp.dma_start(fbq_sb[:, :], fbq.partition_broadcast(128)).then_inc(w_ffn, 16)
            sp.dma_start(fbo_sb[:, :], fbo.partition_broadcast(128)).then_inc(w_ffn, 16)
            sp.dma_start(fbg_sb[:, :], fbg.partition_broadcast(128)).then_inc(w_ffn, 16)
            sp.dma_start(fwo_sb[:, :], fwo).then_inc(w_ffn, 16)
            sp.dma_start(fwg_sb[:, :], fwg).then_inc(w_ffn, 16)
            sp.dma_start(fwe_sb[:, :, :], fwe.rearrange("e d f -> d e f")).then_inc(w_ffn, 16)

            def step(j, p):
                i = 2 * j + p
                load(i + 6, p)
                load_residual(i + 4, p)
                store(i - 1, 1 - p)

            for i in range(-3, 2):
                step(i // 2, i % 2)
            rounds = (NP - 6) // 2
            with sp.Fori(1, rounds) as j:
                step(j, 0)
                step(j, 1)
            for i in range(2 * rounds, NP + 1):
                step(i // 2, i % 2)
            sp.wait_ge(s["stored"], 16 * (NP + 1))
        N_FFN_LOADS = 15

        @block.gpsimd
        def _(pool):
            nc.gpsimd.memset(minus_half[:, :], -0.5)
            nc.gpsimd.memset(ident[:, :], 0.0).then_inc(consts0, 1)
            pool.wait_ge(consts0, 1)
            nc.gpsimd.affine_select(out=ident[:, :], in_=ident[:, :], compare_op=ALU.not_equal, fill=1.0,
                                    base=0, pattern=[[-1, 128]], channel_multiplier=1).then_inc(consts0, 1)
            nc.gpsimd.memset(hide[:, :], 0.0).then_inc(consts0, 1)

            def make_mask():
                pool.wait_ge(consts0, 3)
                for b in range(2):
                    h = hide[b * G:(b + 1) * G, :]
                    nc.gpsimd.affine_select(out=h, in_=h, compare_op=ALU.is_ge, fill=HIDE, base=0,
                                            pattern=[[-1, S]], channel_multiplier=1).then_inc(consts0, 1)
                    pool.wait_ge(consts0, 4 + b)
                nc.gpsimd.tensor_copy(ident_b[:, :], ident[:, :])
                nc.gpsimd.tensor_copy(hide_b[:, :, :], hide[:, :].unsqueeze(1).to_broadcast([128, C, S])).then_inc(consts, 1)

            def outputs(p, nd):
                pool.wait_ge(s["experts_ready"], nd)
                x = expert[p]
                nc.gpsimd.tensor_tensor(x[0:T, 0:4, :], x[0:T, 0:4, :], x[0:T, 4:8, :], ALU.add).then_inc(s["sum4"], 1)
                pool.wait_ge(s["sum4"], nd)
                nc.gpsimd.tensor_tensor(x[0:T, 0:2, :], x[0:T, 0:2, :], x[0:T, 2:4, :], ALU.add).then_inc(s["sum2"], 1)
                pool.wait_ge(s["sum2"], nd)
                nc.gpsimd.tensor_tensor(x[0:T, 0, :], x[0:T, 0, :], x[0:T, 1, :], ALU.add).then_inc(s["sum1"], 1)
                pool.wait_ge(s["sum1"], nd)
                pool.wait_ge(s["base_ready"], nd)
                pool.wait_ge(s["stored"], 16 * (nd))
                nc.gpsimd.tensor_tensor(out_sb[p][0:T, :], x[0:T, 0, :], base[p][0:T, :], ALU.add).then_inc(s["out_ready"], 1)

            def step(j, p):
                i, q = 2 * j + p, 1 - p
                nz, na, nb, nc_, nd = counts(pool, i)
                if isinstance(i, int) and i == -3:
                    make_mask()
                if live(i, 4):
                    wait_alone(pool, "moments1", nz)
                    nc.gpsimd.tensor_scalar(ve1[p][0:T, :], mv1[p][0:T, 1:2], LN_EPS, 1.0, ALU.add, ALU.mult).then_inc(s["var1"], 1)
                    pool.wait_ge(s["var1"], nz)
                    nc.gpsimd.tensor_tensor(rstd1[p][0:T, :], ve1[p][0:T, :], minus_half[0:T, 0:1], ALU.pow).then_inc(s["rstd1_ready"], 1)
                if live(i, 1):
                    pool.wait_ge(s["kv_ready"], nc_)
                    pool.wait_ge(s["fq_ready"], nc_)
                    nc.gpsimd.tensor_tensor(
                        prod1[0:T, 0:HP, :, :],
                        fkv[q][0:T, 0, :].rearrange("p (g d) -> p g d", g=FH).unsqueeze(1).to_broadcast([T, HP, FH, FD]),
                        fq[q][0:T, 0:HP * FD].rearrange("p (h d) -> p h d", h=HP).unsqueeze(2).to_broadcast([T, HP, FH, FD]),
                        ALU.mult).then_inc(s["prod1_pool"], 1)
                if live(i, 0):
                    wait_alone(pool, "ssq_ready", nd)
                    nc.gpsimd.tensor_scalar(ms[p][0:T, :], ssq[p][0:T, :], 1.0 / D, RMS_EPS, ALU.mult, ALU.add).then_inc(s["ms_ready"], 1)
                    pool.wait_ge(s["ms_ready"], nd)
                    nc.gpsimd.tensor_tensor(r2[p][0:T, :], ms[p][0:T, :], minus_half[0:T, 0:1], ALU.pow).then_inc(s["r2_ready"], 1)
                    wait_alone(pool, "r2_ready", nd)
                    nc.gpsimd.tensor_scalar(r2g[p][0:T, :], r2[p][0:T, :], gates[0:T, 1:2], 1.0, ALU.mult, ALU.mult).then_inc(s["r2g_ready"], 1)
                    if not (isinstance(i, int) and i == 0):
                        outputs(q, nd - 1)
                    wait_alone(pool, "ginv_ready", nd)
                    pool.wait_ge(s["r2g_ready"], nd)
                    nc.gpsimd.tensor_scalar(gate[p][0:T, :], gexp[p][0:T, :], ginv[p][0:T, :], r2g[p][0:T, :], ALU.mult, ALU.mult).then_inc(s["gate_ready"], 1)
                if live(i, 2):
                    wait_alone(pool, "moments2", nb)
                    nc.gpsimd.tensor_scalar(ve2[p][0:T, 0:1], mv2[p][0:T, 1:2], LN_EPS, 1.0, ALU.add, ALU.mult).then_inc(s["var2a"], 1)
                    wait_alone(pool, "var2a", nb)
                    nc.gpsimd.tensor_scalar(ve2[p][0:T, 1:2], ve2[p][0:T, 0:1], RMS_EPS, mv2[p][0:T, 1:2], ALU.mult, ALU.add).then_inc(s["var2b"], 1)
                    pool.wait_ge(s["var2b"], nb)
                    nc.gpsimd.tensor_tensor(rstd2[p][0:T, :], ve2[p][0:T, :], minus_half[0:T, :], ALU.pow).then_inc(s["rstd2_ready"], 1)
                if live(i, 3):
                    pool.wait_ge(s["prinv_ready"], na)
                    nc.gpsimd.tensor_tensor(probs[q][0:TG, :, :, 0:S], probs[q][0:TG, :, :, 0:S],
                                            prinv[q][0:TG, :, :].unsqueeze(3).to_broadcast([TG, C, 2, S]),
                                            ALU.mult).then_inc(s["probs_ready"], 1)
                if live(i, 2):
                    wait_alone(pool, "rstd2_ready", nb)
                    nc.gpsimd.tensor_scalar(u_sb[p][0:T, :], x1[p][0:T, :], mv2[p][0:T, 0:1], rstd2[p][0:T, 0:1],
                                            ALU.subtract, ALU.mult).then_inc(s["u_ready"], 1)
                    pool.wait_ge(s["u_ready"], nb)
                    nc.gpsimd.tensor_tensor(ub_sb[p][0:T, :], u_sb[p][0:T, :], fbo_sb[0:T, :], ALU.add).then_inc(s["ub_ready"], 1)

            run(pool, step)
            outputs((NP - 1) % 2, NP)

        @block.scalar
        def _(act):
            act.dma_start(wq_sb[:, :, :], wq.rearrange("d (c f) -> d c f", c=C)).then_inc(wq_loaded, 16)
            act.dma_start(wk_sb[:, :, :], wk.rearrange("d (c f) -> d c f", c=C)).then_inc(wk_loaded, 16)
            act.wait_ge(consts0, 1)
            nc.scalar.activation(x2sq[:, 0:1], minus_half[:, 0:1], ACT.Exp)
            act.wait_ge(pads_zeroed, 2)

            def chunks(dst, src, done, n, width, ready):
                for half in range(2):
                    if half < len(done):
                        act.wait_ge(s[done[half]], n)
                    last = nc.scalar.copy(dst[:, half * HC:(half + 1) * HC, :],
                                          src[:, half, 0:HC * width].rearrange("p (c s) -> p c s", c=HC))
                last.then_inc(s[ready], 1)

            def step(j, p):
                i, q = 2 * j + p, 1 - p
                nz, na, nb, nc_, nd = counts(act, i)
                if isinstance(i, int) and i == -2:
                    act.wait_ge(w_ffn, 16 * N_FFN_LOADS)
                    nc.scalar.activation(gates[:, :], gates_in[:, :], ACT.Tanh).then_inc(gates_ready, 1)
                if live(i, 1):
                    act.wait_ge(s["h_turned"], nc_)
                    nc.scalar.copy(hT[q][:, :], ps_x[:, 0:T]).then_inc(s["hT_ready"], 1)
                if live(i, 3):
                    chunks(qT[q], ps_qkv, ("q_lo", "q_hi"), na, T, "qT_ready")
                if live(i, 1):
                    act.wait_ge(s["c_made"], nc_)
                    nc.scalar.activation(cT[q][0:L, :], ps_kv[0:L, 0:T], ACT.Identity, bias=fbdown_sb[0:L, :]).then_inc(s["cT_ready"], 1)
                if live(i, 2):
                    for half, done in enumerate(("p_lo", "p_hi")):
                        act.wait_ge(s[done], nb)
                        last = nc.scalar.copy(
                            probsT[p][:, half * HC:(half + 1) * HC, :].rearrange("p c (b s) -> p c b s", b=2),
                            ps_pa[:, half, :].rearrange("p (c b s) -> p c b s", c=HC, b=2)[:, :, :, 0:S])
                    last.then_inc(s["probsT_ready"], 1)
                if live(i, 1):
                    act.wait_ge(s["kv_made"], nc_)
                    nc.scalar.copy(fkv[q][0:T, :, :], ps_kv[0:T, 0:2 * D].rearrange("p (n f) -> p n f", n=2)).then_inc(s["kv_ready"], 1)
                if live(i, 0):
                    act.wait_ge(s["o_turned"], nd)
                    nc.scalar.copy(oT[p][:, :], ps_x[:, 0:T]).then_inc(s["oT_ready"], 1)
                if live(i, 3):
                    chunks(kT[q], ps_qkv, ("k_lo", "k_hi"), na, T, "kT_ready")
                if live(i, 0):
                    act.wait_ge(s["x2_ready"], nd)
                    nc.scalar.activation(x2sq[0:T, :], x2[p][0:T, :], ACT.Square, accum_out=ssq[p][0:T, :]).then_inc(s["ssq_ready"], 1)
                if live(i, 0):
                    act.wait_ge(s["x2_turned"], nd)
                    nc.scalar.copy(x2T[p][:, :], ps_x[:, 0:T]).then_inc(s["x2T_ready"], 1)
                if live(i, 2):
                    chunks(attnT[p], ps_pa, ("a_made",), nb, T, "attnT_ready")
                if live(i, 1):
                    act.wait_ge(s["lshift_ready"], nc_)
                    nc.scalar.activation(ps_kv[0:T, 2 * D:4 * D], lshift[q][0:T, :, :].rearrange("p h g -> p (h g)"), ACT.Exp,
                                         scale=float(FD) ** -0.5).then_inc(s["e_ready"], 1)
                if live(i, 3):
                    act.wait_ge(s["v_made"], na)
                    nc.scalar.copy(v_sb[q][:, :, :, :].rearrange("p b c e -> p b (c e)"), ps_qkv[:, :, :]).then_inc(s["v_ready"], 1)
                if live(i, 4):
                    act.wait_ge(s["xc_turned"], nz)
                    nc.scalar.copy(xcT[p][:, :, 0:T], ps_x[:, 0:256].rearrange("p (n s) -> p n s", n=2)[:, :, 0:T]).then_inc(s["xcT_ready"], 1)
                if live(i, 0):
                    act.wait_ge(s["gmax_ready"], nd)
                    nc.scalar.activation(gexp[p][0:T, :], glog[p][0:T, :], ACT.Exp, bias=gmax[p][0:T, :],
                                         accum_out=gsum[p][0:T, :]).then_inc(s["gexp_ready"], 1)
                if live(i, 3):
                    act.wait_ge(s["scores_shifted"], na)
                    nc.scalar.activation(probs[q][0:TG, :, :, 0:S].rearrange("p c r k -> p r c k"),
                                         ps_se[0:TG, :, 0:C * S].rearrange("p r (c k) -> p r c k", c=C), ACT.Exp,
                                         scale=float(DK) ** -0.5).then_inc(s["probs_exp"], 1)
                if live(i, 0):
                    act.wait_ge(s["gate_ready"], nd)
                    for e in range(E):
                        if e % 4 == 0:
                            act.wait_ge(s["experts_made"], nd + nd - 1 + e // 4)
                        last = nc.scalar.activation(expert[p][0:T, e, :], ps_pa[0:T, e // 4, (e % 4) * D:(e % 4 + 1) * D],
                                                    ACT.Copy, scale=gate[p][0:T, e:e + 1])
                    last.then_inc(s["experts_ready"], 1)

            run(act, step)

        @block.vector
        def _(dve):
            for p in range(2):
                nc.vector.memset(xcT[p][:, :, :], 0.0)
            for p in range(2):
                nc.vector.memset(probs[p][:, :, :, :], 0.0).then_inc(pads_zeroed, 1)
            for p in range(2):
                ins = nc.vector.memset(cT[p][L:L + 1, :], 1.0)
            ins.then_inc(s["stored"], 16)

            def scale_weights():
                dve.wait_ge(w_ffn, 16 * N_FFN_LOADS)
                nc.vector.tensor_scalar(fwq_sb[:, :], fwq_sb[:, :], gam[:, 0:1], None, ALU.mult)
                nc.vector.tensor_scalar(fwdown_sb[:, :], fwdown_sb[:, :], gam[:, 0:1], None, ALU.mult)
                nc.vector.tensor_scalar(fwg_sb[:, :], fwg_sb[:, :], gam[:, 1:2], None, ALU.mult)
                nc.vector.tensor_scalar(fwe_sb[:, :, :], fwe_sb[:, :, :], gam[:, 1:2], None, ALU.mult)
                up = fwup_in[0:L + 1, :].rearrange("p (h n d) -> p h n d", h=FH, n=2)
                nc.vector.tensor_copy(fwup_sb[0:L + 1, 0, :].rearrange("p (h d) -> p h d", h=FH), up[:, :, 0, :])
                nc.vector.tensor_copy(fwup_sb[0:L + 1, 1, :].rearrange("p (d h) -> p h d", h=FH), up[:, :, 1, :]).then_inc(scaled, 1)
                dve.wait_ge(gates_ready, 1)

            def step(j, p):
                i, q = 2 * j + p, 1 - p
                nz, na, nb, nc_, nd = counts(dve, i)
                if isinstance(i, int) and i == -2:
                    scale_weights()
                if live(i, 0):
                    wait_prod2 = s["prod2_ready"]
                    dve.wait_ge(wait_prod2, nd)
                    nc.vector.tensor_reduce(oraw[p][0:T, :, :], prod2[0:T, :, :, :], AX.X, ALU.add).then_inc(s["oraw_ready"], 1)
                    dve.wait_ge(s["oraw_ready"], nd)
                    dve.wait_ge(s["einv_ready"], nd)
                    nc.vector.tensor_tensor(onorm[p][0:T, :].rearrange("p (h d) -> p h d", h=FH), oraw[p][0:T, :, :],
                                            einv[p][0:T, :].unsqueeze(2).to_broadcast([T, FH, FD]), ALU.mult).then_inc(s["onorm_ready"], 1)
                if live(i, 1):
                    dve.wait_ge(s["fq_made"], nc_)
                    nc.vector.tensor_tensor(fq[q][0:T, :], ps_x[0:T, 0:D], fbq_sb[0:T, :], ALU.add).then_inc(s["fq_ready"], 1)
                if live(i, 4):
                    dve.wait_ge(x_loaded[p], 16 * (j + 3))
                    nc.vector.bn_stats(st1[p][0:T, :], x_sb[p][0:T, :]).then_inc(s["stats1"], 1)
                    wait_alone(dve, "stats1", nz)
                    nc.vector.bn_aggr(mv1[p][0:T, :], st1[p][0:T, :]).then_inc(s["moments1"], 1)
                if live(i, 1):
                    dve.wait_ge(s["kv_ready"], nc_)
                    dve.wait_ge(s["fq_ready"], nc_)
                    nc.vector.tensor_tensor(
                        prod1[0:T, HP:FH, :, :],
                        ps_kv[0:T, 0:D].rearrange("p (g d) -> p g d", g=FH).unsqueeze(1).to_broadcast([T, FH - HP, FH, FD]),
                        fq[q][0:T, HP * FD:D].rearrange("p (h d) -> p h d", h=FH - HP).unsqueeze(2).to_broadcast([T, FH - HP, FH, FD]),
                        ALU.mult).then_inc(s["prod1_ready"], 1)
                if live(i, 0):
                    dve.wait_ge(s["o_made"], nd)
                    dve.wait_ge(s["ub_ready"], nd)
                    nc.vector.tensor_tensor(x2[p][0:T, :], ps_x[0:T, 0:D], ub_sb[p][0:T, :], ALU.add).then_inc(s["x2_ready"], 1)
                if live(i, 4):
                    dve.wait_ge(s["rstd1_ready"], nz)
                    nc.vector.tensor_scalar(xln[p][0:T, :], x_sb[p][0:T, :], mv1[p][0:T, 0:1], rstd1[p][0:T, :],
                                            ALU.subtract, ALU.mult).then_inc(s["xln_ready"], 1)
                if live(i, 1):
                    dve.wait_ge(s["prod1_pool"], nc_)
                    dve.wait_ge(s["prod1_ready"], nc_)
                    nc.vector.tensor_reduce(logit[q][0:T, :, :], prod1[0:T, :, :, :], AX.X, ALU.add).then_inc(s["logit_ready"], 1)
                if live(i, 0):
                    dve.wait_ge(s["x2_ready"], nd)
                    nc.vector.scalar_tensor_tensor(out=base[p][0:T, :], in0=x2[p][0:T, :], scalar=gates[0:T, 1:2],
                                                   in1=x1[p][0:T, :], op0=ALU.mult, op1=ALU.add).then_inc(s["base_ready"], 1)
                if live(i, 0):
                    dve.wait_ge(s["glog_made"], nd)
                    dve.wait_ge(s["r2_ready"], nd)
                    nc.vector.scalar_tensor_tensor(out=glog[p][0:T, :], in0=ps_x[0:T, 256:256 + E], scalar=r2[p][0:T, :],
                                                   in1=fbg_sb[0:T, :], op0=ALU.mult, op1=ALU.add).then_inc(s["glog_ready"], 1)
                    dve.wait_ge(s["glog_ready"], nd)
                    nc.vector.tensor_reduce(gmax[p][0:T, :], glog[p][0:T, :], AX.X, ALU.max, negate=True).then_inc(s["gmax_ready"], 1)
                if live(i, 1):
                    dve.wait_ge(s["logit_ready"], nc_)
                    nc.vector.tensor_reduce(lmax[q][0:T, :], logit[q][0:T, :, :], AX.X, ALU.max).then_inc(s["lmax_ready"], 1)
                    dve.wait_ge(s["lmax_ready"], nc_)
                    nc.vector.tensor_tensor(lshift[q][0:T, :, :], logit[q][0:T, :, :],
                                            lmax[q][0:T, :].unsqueeze(2).to_broadcast([T, FH, FH]),
                                            ALU.subtract).then_inc(s["lshift_ready"], 1)
                if live(i, 1):
                    dve.wait_ge(s["e_ready"], nc_)
                    nc.vector.tensor_reduce(esum[q][0:T, :], ps_kv[0:T, 2 * D:4 * D].rearrange("p (h g) -> p h g", h=FH),
                                            AX.X, ALU.add).then_inc(s["esum_ready"], 1)
                    nc.vector.tensor_tensor(
                        prod2[0:T, :, :, :],
                        ps_kv[0:T, 2 * D:4 * D].rearrange("p (h g) -> p h g", h=FH).unsqueeze(2).to_broadcast([T, FH, FD, FH]),
                        fkv[q][0:T, 1, :].rearrange("p (d g) -> p d g", d=FD).unsqueeze(1).to_broadcast([T, FH, FD, FH]),
                        ALU.mult).then_inc(s["prod2_ready"], 1)
                    dve.wait_ge(s["esum_ready"], nc_)
                    nc.vector.reciprocal(einv[q][0:T, :], esum[q][0:T, :]).then_inc(s["einv_ready"], 1)
                if live(i, 3):
                    dve.wait_ge(s["scores_made"], na)
                    nc.vector.tensor_reduce(nmax[q][0:TG, :, :], ps_se[0:TG, :, 0:C * S].rearrange("p r (c k) -> p r c k", c=C),
                                            AX.X, ALU.max, negate=True).then_inc(s["nmax_ready"], 1)
                if live(i, 0):
                    dve.wait_ge(s["gexp_ready"], nd)
                    nc.vector.reciprocal(ginv[p][0:T, :], gsum[p][0:T, :]).then_inc(s["ginv_ready"], 1)
                if live(i, 2):
                    dve.wait_ge(s["y_made"], nb)
                    dve.wait_ge(xres_loaded[p], 16 * (j + 2))
                    nc.vector.scalar_tensor_tensor(out=x1[p][0:T, :], in0=ps_x[0:T, 0:D], scalar=gates[0:T, 0:1],
                                                   in1=xres[p][0:T, :], op0=ALU.mult, op1=ALU.add).then_inc(s["x1_ready"], 1)
                    dve.wait_ge(s["x1_ready"], nb)
                    nc.vector.bn_stats(st2[p][0:T, :], x1[p][0:T, :]).then_inc(s["stats2"], 1)
                    wait_alone(dve, "stats2", nb)
                    nc.vector.bn_aggr(mv2[p][0:T, :], st2[p][0:T, :]).then_inc(s["moments2"], 1)
                if live(i, 3):
                    dve.wait_ge(s["probs_exp"], na)
                    nc.vector.tensor_reduce(psums[q][0:TG, :, :], probs[q][0:TG, :, :, 0:S], AX.X, ALU.add).then_inc(s["psum_ready"], 1)
                    dve.wait_ge(s["psum_ready"], na)
                    nc.vector.reciprocal(prinv[q][0:TG, :, :], psums[q][0:TG, :, :]).then_inc(s["prinv_ready"], 1)
                if live(i, 2):
                    dve.wait_ge(s["rstd2_ready"], nb)
                    nc.vector.tensor_scalar(h_sb[p][0:T, :], x1[p][0:T, :], mv2[p][0:T, 0:1], rstd2[p][0:T, 1:2],
                                            ALU.subtract, ALU.mult).then_inc(s["h_ready"], 1)

            run(dve, step)

        @block.tensor
        def _(pe):
            pe.wait_ge(consts0, 2)

            for _i in range(WARM_UP):
                nc.tensor.matmul(ps_se[:, 0, 0:128], ident[:, :], ident[:, :], start=True, stop=True)

            def mm(o, lhsT, rhs, start=True, stop=True):
                return nc.tensor.matmul(o, lhsT, rhs, start=start, stop=stop, skip_group_check=True)

            def project(dst, w, rhs, half, done):
                for ch in range(half * HC, (half + 1) * HC):
                    ins = mm(dst[:, half, ch % HC * T:(ch % HC + 1) * T], w[:, ch, :], rhs)
                ins.then_inc(s[done], 1)

            def step(j, p):
                i, q = 2 * j + p, 1 - p
                nz, na, nb, nc_, nd = counts(pe, i)
                if isinstance(i, int) and i == -3:
                    pe.wait_ge(wq_loaded, 16)
                if isinstance(i, int) and i == -1:
                    pe.wait_ge(scaled, 1)
                if live(i, 3):
                    pe.wait_ge(s["xcT_ready"], na)
                    if live(i, 2):
                        pe.wait_ge(s["v_ready"], nb)
                    project(ps_qkv, wq_sb, xcT[q][:, 0, 0:T], 0, "q_lo")
                if live(i, 1):
                    pe.wait_ge(s["h_ready"], nc_)
                    nc.tensor.transpose(ps_x[:, 0:T], h_sb[q][0:T, :], ident[0:T, 0:T]).then_inc(s["h_turned"], 1)
                if live(i, 3):
                    project(ps_qkv, wq_sb, xcT[q][:, 0, 0:T], 1, "q_hi")
                if live(i, 1):
                    pe.wait_ge(s["hT_ready"], nc_)
                    mm(ps_x[0:T, 0:D], hT[q][:, :], fwq_sb[:, :]).then_inc(s["fq_made"], 1)
                    if live(i, 0):
                        pe.wait_ge(s["prod2_ready"], nd)
                    mm(ps_kv[0:L, 0:T], fwdown_sb[:, :], hT[q][:, :]).then_inc(s["c_made"], 1)
                if live(i, 2):
                    pe.wait_ge(s["probs_ready"], nb)
                    if live(i, -1) and not (isinstance(i, int) and i < 1):
                        pe.wait_ge(s["experts_ready"], nd - 1)
                    elif live(i, 1):
                        pe.wait_ge(s["attnT_ready"], nc_)
                    for ch in range(C):
                        ins = nc.tensor.transpose(ps_pa[:, ch // HC, ch % HC * 128:ch % HC * 128 + TG],
                                                  probs[p][0:TG, ch, :, :].rearrange("p r k -> p (r k)"), ident[0:TG, 0:TG])
                        if ch % HC == HC - 1:
                            ins.then_inc(s["p_hi" if ch // HC else "p_lo"], 1)
                if live(i, 1):
                    pe.wait_ge(s["cT_ready"], nc_)
                    mm(ps_kv[0:T, 0:2 * D], cT[q][0:L + 1, :], fwup_sb[0:L + 1, :, :].rearrange("p n f -> p (n f)")).then_inc(s["kv_made"], 1)
                if live(i, 0):
                    pe.wait_ge(s["onorm_ready"], nd)
                    if live(i, 1):
                        pe.wait_ge(s["fq_ready"], nc_)
                    else:
                        pe.wait_ge(s["glog_ready"], nd - 1)
                    nc.tensor.transpose(ps_x[:, 0:T], onorm[p][0:T, :], ident[0:T, 0:T]).then_inc(s["o_turned"], 1)
                if live(i, 3):
                    if isinstance(i, int) and i == -3:
                        pe.wait_ge(wk_loaded, 16)
                    pe.wait_ge(s["qT_ready"], na)
                    project(ps_qkv, wk_sb, xcT[q][:, 1, 0:T], 0, "k_lo")
                    project(ps_qkv, wk_sb, xcT[q][:, 1, 0:T], 1, "k_hi")
                if live(i, 0):
                    pe.wait_ge(s["oT_ready"], nd)
                    mm(ps_x[0:T, 0:D], oT[p][:, :], fwo_sb[:, :]).then_inc(s["o_made"], 1)
                for k in range(C):
                    if live(i, 2):
                        if k == 0:
                            wait_alone(pe, "probsT_ready", nb)
                        for r in range(2):
                            ch = (k + r * HC) % C
                            for bt in range(2):
                                ins = mm(ps_pa[r * G:r * G + DK, ch // HC, ch % HC * T + bt * S:ch % HC * T + (bt + 1) * S],
                                         v_sb[p][r * G:r * G + S, bt, ch, :], probsT[p][r * G:r * G + S, ch, bt * S:(bt + 1) * S])
                        if k == C - 1:
                            ins.then_inc(s["a_made"], 1)
                    if live(i, 0) and k == HC - 1:
                        pe.wait_ge(s["x2_ready"], nd)
                        nc.tensor.transpose(ps_x[:, 0:T], x2[p][0:T, :], ident[0:T, 0:T]).then_inc(s["x2_turned"], 1)
                if live(i, 0):
                    pe.wait_ge(s["x2T_ready"], nd)
                    mm(ps_x[0:T, 256:256 + E], x2T[p][:, :], fwg_sb[:, :]).then_inc(s["glog_made"], 1)
                if live(i, 3):
                    if isinstance(i, int) and i == -3:
                        pe.wait_ge(wv_loaded, 32)
                    pe.wait_ge(s["kT_ready"], na)
                    for bt in range(2):
                        for r in range(2):
                            ins = mm(ps_qkv[r * G:(r + 1) * G, bt, :], xcT[q][:, 1, bt * S:bt * S + G],
                                     wv_sb[:, r, :, :].rearrange("p c e -> p (c e)"))
                    ins.then_inc(s["v_made"], 1)
                if live(i, 4):
                    pe.wait_ge(s["xln_ready"], nz)
                    pe.wait_ge(ctx_loaded[p], 32 * (j + 3))
                    if live(i, 0):
                        pe.wait_ge(s["glog_ready"], nd)
                    elif live(i, 1):
                        pe.wait_ge(s["fq_ready"], nc_)
                    elif i > -4:
                        pe.wait_ge(s["xcT_ready"], nz - 1)
                    nc.tensor.transpose(ps_x[:, 0:T], xln[p][0:T, :], ident[0:T, 0:T])
                    nc.tensor.transpose(ps_x[:, 128:128 + T], ctx_sb[p][0:T, :], ident[0:T, 0:T]).then_inc(s["xc_turned"], 1)
                if live(i, 3):
                    if isinstance(i, int) and i == -3:
                        pe.wait_ge(consts, 1)
                    for r in range(2):
                        mm(ps_se[0:TG, r, 0:C * S], ident_b[0:TG, 0:TG], hide_b[0:TG, :, :].rearrange("p c k -> p (c k)"), stop=False)
                    for ch in range(C):
                        for r in range(2):
                            for bt in range(2):
                                ins = mm(ps_se[bt * G:bt * G + S, r, ch * S:(ch + 1) * S],
                                         qT[q][r * G:(r + 1) * G, ch, bt * S:(bt + 1) * S],
                                         kT[q][r * G:(r + 1) * G, ch, bt * S:(bt + 1) * S], start=False, stop=False)
                    ins.then_inc(s["scores_made"], 1)
                if live(i, 2):
                    if isinstance(i, int) and i == -2:
                        pe.wait_ge(wo_loaded, 16)
                    pe.wait_ge(s["attnT_ready"], nb)
                    if live(i, 4):
                        pe.wait_ge(s["xcT_ready"], nz)
                    elif live(i, 0):
                        pe.wait_ge(s["glog_ready"], nd)
                    for ch in range(C):
                        ins = mm(ps_x[0:T, 0:D], attnT[p][:, ch, :], wo_sb[:, ch, :], start=(ch == 0), stop=(ch == C - 1))
                    ins.then_inc(s["y_made"], 1)
                if live(i, 3):
                    pe.wait_ge(s["nmax_ready"], na)
                    for r in range(2):
                        ins = mm(ps_se[0:TG, r, 0:C * S], ident_b[0:TG, 0:TG],
                                 nmax[q][0:TG, r, :].unsqueeze(2).to_broadcast([TG, C, S]), start=False)
                    ins.then_inc(s["scores_shifted"], 1)
                if live(i, 0):
                    if not live(i, 2):
                        pe.wait_ge(s["experts_ready"], nd - 1)
                    for n in range(2):
                        mm(ps_pa[0:T, n, :], x2T[p][:, :],
                           fwe_sb[:, n * 4:(n + 1) * 4, :].rearrange("p e f -> p (e f)")).then_inc(s["experts_made"], 1)

            run(pe, step)


_INS = ["x", "ctx_1024", "g_xattn", "g_ffn", "L0_xattn_Wq", "L0_xattn_Wk", "L0_xattn_Wv", "L0_xattn_Wo",
        "L0_ffn_gamma1", "L0_ffn_Wq", "L0_ffn_bq", "L0_ffn_Wdown", "L0_ffn_bdown", "L0_ffn_Wup", "L0_ffn_bup",
        "L0_ffn_Wo", "L0_ffn_bo", "L0_ffn_gamma2", "L0_ffn_Wg", "L0_ffn_bg", "L0_ffn_We"]


def kernel(**inputs):
    import concourse.bacc as bacc
    from concourse.bass_utils import run_bass_kernel_spmd

    nc = bacc.Bacc("TRN2", target_bir_lowering=False, num_devices=1)
    arrays, args = {}, []
    for name in _INS:
        a = np.ascontiguousarray(inputs[name])
        arrays[f"in_{name}"] = a
        args.append(nc.dram_tensor(f"in_{name}", a.shape, mybir.dt.from_np(a.dtype), kind="ExternalInput").ap())
    out = nc.dram_tensor("out", inputs["x"].shape, F32, kind="ExternalOutput").ap()
    build(nc, *args, out)
    r = run_bass_kernel_spmd(nc, [arrays], core_ids=[0])
    return r.results[0]["out"]
```

```python
from contextlib import ExitStack

import numpy as np

import concourse.bass as bass
from concourse import mybir

ALU = mybir.AluOpType
ACT = mybir.ActivationFunctionType
AX = mybir.AxisListType
F32 = mybir.dt.float32
BF16 = mybir.dt.bfloat16

HP = 5
WARM_UP = 7
NC = 3
HIDE = -1e30
LN_EPS = 1e-5
RMS_EPS = 1e-6


def build(nc, x, ctx_kv, g_xattn, g_ffn, wq, wk, wv, wo, gamma1, fwq, fbq, fwdown, fbdown, fwup, fbup,
          fwo, fbo, gamma2, fwg, fbg, fwe, out):
    B, S, D = x.shape
    DK = 64
    H = wq.shape[1] // DK
    C = H // 2
    NP = B // 2
    T = 2 * S
    G = 64
    TG = G + S
    L = fwdown.shape[1]
    FH = 16
    FD = D // FH
    E = fwg.shape[1]
    HC = C // 2
    assert D == 128 and H * DK == C * 128 and fwup.shape[1] == 2 * D and T <= 128

    x_pairs = x.rearrange("(n b) s d -> n (b s) d", b=2)
    out_pairs = out.rearrange("(n b) s d -> n (b s) d", b=2)
    ctx_pairs = ctx_kv.rearrange("(n b) s d -> n b s d", b=2)

    with ExitStack() as stack:
        def sb(name, shape, dt=F32):
            return stack.enter_context(nc.sbuf_tensor(name, shape, dt))

        def two(name, shape, dt=F32):
            return [sb(f"{name}_{i}", shape, dt) for i in range(2)]

        def sem(name):
            return stack.enter_context(nc.semaphore(name))

        ps_qkv = stack.enter_context(nc.psum_tensor("ps_qkv", [128, 2, 512], F32))
        ps_pa = stack.enter_context(nc.psum_tensor("ps_pa", [128, 2, 512], F32))
        ps_se = stack.enter_context(nc.psum_tensor("ps_se", [128, 2, 512], F32))
        ps_x = stack.enter_context(nc.psum_tensor("ps_x", [128, 512], F32))
        ps_kv = stack.enter_context(nc.psum_tensor("ps_kv", [128, 512], F32))

        ident = sb("ident", [128, 128])
        ident_b = sb("ident_b", [128, 128], BF16)
        hide = sb("hide", [128, S])
        hide_b = sb("hide_b", [128, C, S], BF16)
        minus_half = sb("minus_half", [128, 2])
        wq_sb = sb("wq_sb", [128, C, 128])
        wk_sb = sb("wk_sb", [128, C, 128])
        wv_sb = sb("wv_sb", [128, 2, C, DK])
        wo_sb = sb("wo_sb", [128, C, D])
        gam = sb("gam", [128, 2])
        fwq_sb = sb("fwq_sb", [128, D])
        fwdown_sb = sb("fwdown_sb", [128, L])
        fbdown_sb = sb("fbdown_sb", [128, 1])
        fwup_in = sb("fwup_in", [128, 2 * D])
        fwup_sb = sb("fwup_sb", [128, 2, D])
        fwo_sb = sb("fwo_sb", [128, D])
        fwg_sb = sb("fwg_sb", [128, E])
        fwe_sb = sb("fwe_sb", [128, E, D])
        fbq_sb = sb("fbq_sb", [128, D])
        fbo_sb = sb("fbo_sb", [128, D])
        fbg_sb = sb("fbg_sb", [128, E])
        gates_in = sb("gates_in", [128, 2])
        gates = sb("gates", [128, 2])

        x_sb = two("x_sb", [128, D])
        xres = two("xres", [128, D])
        ctx_sb = two("ctx_sb", [128, D])
        st1 = two("st1", [128, 6])
        mv1 = two("mv1", [128, 2])
        ve1 = two("ve1", [128, 1])
        rstd1 = two("rstd1", [128, 1])
        xln = two("xln", [128, D])
        xcT = two("xcT", [128, 2, 120])
        qT = two("qT", [128, C, T])
        kT = two("kT", [128, C, 2, 2, S])
        v_sb = two("v_sb", [128, 2, C, DK])
        nmax = two("nmax", [128, 2, C], BF16)
        probs = two("probs", [128, C, 2, G])
        psums = two("psums", [128, C, 2])
        prinv = two("prinv", [128, C, 2])
        probsT = two("probsT", [128, C, T])
        attnT = two("attnT", [128, C, T])
        x1 = two("x1", [128, D])
        st2 = two("st2", [128, 6])
        mv2 = two("mv2", [128, 2])
        ve2 = two("ve2", [128, 2])
        rstd2 = two("rstd2", [128, 2])
        u_sb = two("u_sb", [128, D])
        h_sb = two("h_sb", [128, D])
        ub_sb = two("ub_sb", [128, D])
        hT = two("hT", [128, T])
        cT = two("cT", [128, T])
        fq = two("fq", [128, D])
        fkv = two("fkv", [128, 2, D])
        prod1 = sb("prod1", [128, FH, FH, FD])
        prod2 = sb("prod2", [128, FH, FD, FH])
        logit = two("logit", [128, FH, FH])
        lmax = two("lmax", [128, FH])
        lshift = two("lshift", [128, FH, FH])
        esum = two("esum", [128, FH])
        einv = two("einv", [128, FH])
        oraw = two("oraw", [128, FH, FD])
        onorm = two("onorm", [128, D])
        oT = two("oT", [128, T])
        x2 = two("x2", [128, D])
        x2sq = sb("x2sq", [128, D])
        ssq = two("ssq", [128, 1])
        ms = two("ms", [128, 1])
        r2 = two("r2", [128, 1])
        r2g = two("r2g", [128, 1])
        x2T = two("x2T", [128, T])
        glog = two("glog", [128, E])
        gmax = two("gmax", [128, 1])
        gexp = two("gexp", [128, E])
        gsum = two("gsum", [128, 1])
        ginv = two("ginv", [128, 1])
        gate = two("gate", [128, E])
        base = two("base", [128, D])
        expert = two("expert", [128, E, D])
        out_sb = two("out_sb", [128, D])
        out_last = sb("out_last", [128, D])

        wq_loaded = sem("wq_loaded")
        wk_loaded = sem("wk_loaded")
        wv_loaded = sem("wv_loaded")
        wo_loaded = sem("wo_loaded")
        w_ffn = sem("w_ffn")
        consts0 = sem("consts0")
        consts = sem("consts")
        pads_zeroed = sem("pads_zeroed")
        scaled = sem("scaled")
        gates_ready = sem("gates_ready")
        names = """xln_ready stats1 moments1 var1 rstd1_ready xc_turned xcT_ready
            q_lo q_hi qT_ready k_lo k_hi kT_ready v_made v_ready scores_made nmax_ready scores_shifted
            probs_exp psum_ready prinv_ready probs_pool probs_ready p_lo p_hi probsT_ready a_made attnT_ready y_made
            x1_ready stats2 moments2 var2 rstd2_ready u_ready h_ready ub_ready h_turned hT_ready
            fq_made fq_ready c_made cT_ready kv_made kv_ready prod1_pool prod1_ready logit_ready lmax_ready
            lshift_ready e_ready esum_ready einv_ready prod2_ready oraw_ready onorm_ready o_turned oT_ready
            o_made x2_ready ssq_ready ms_ready r2_ready r2g_ready x2_turned x2T_ready glog_made glog_ready gmax_ready
            gexp_ready ginv_ready gate_ready experts_made base_ready experts_ready sum4 sum2 sum1 out_ready
            last_half last_sum4 last_sum2 last_sum1 last_out stored"""
        x_loaded = [sem(f"x_loaded_{i}") for i in range(2)]
        ctx_loaded = [sem(f"ctx_loaded_{i}") for i in range(2)]
        xres_loaded = [sem(f"xres_loaded_{i}") for i in range(2)]
        s = {n: sem(n) for n in names.split()}

        block = stack.enter_context(nc.Block())

        def run(eng, step):
            for i in range(-4, 2):
                step(i // 2, i % 2)
            rounds = (NP - 4) // 2
            with eng.Fori(1, rounds) as j:
                step(j, 0)
                step(j, 1)
            for i in range(2 * rounds, NP):
                step(i // 2, i % 2)

        def live(i, ahead):
            return not isinstance(i, int) or 0 <= i + ahead < NP

        def k_banks(i):
            return ps_pa if isinstance(i, int) and i == -3 else ps_qkv

        def counts(eng, i):
            n = (i + 5, i + 4, i + 3, i + 2, i + 1)
            if not isinstance(i, int):
                for v in n:
                    eng.to_reg(v)
            return n

        def wait_alone(eng, name, value):
            eng.wait_ge(consts0, 1)
            eng.wait_ge(s[name], value)

        def outputs(eng, ops, p, n, last=False):
            sums = ["last_sum4", "last_sum2", "last_sum1", "last_out"] if last else ["sum4", "sum2", "sum1", "out_ready"]
            done = 1 if last else n
            eng.wait_ge(s["experts_ready"], n)
            x = expert[p]
            ops.tensor_tensor(x[0:T, 0:4, :], x[0:T, 0:4, :], x[0:T, 4:8, :], ALU.add).then_inc(s[sums[0]], 1)
            eng.wait_ge(s[sums[0]], done)
            ops.tensor_tensor(x[0:T, 0:2, :], x[0:T, 0:2, :], x[0:T, 2:4, :], ALU.add).then_inc(s[sums[1]], 1)
            eng.wait_ge(s[sums[1]], done)
            ops.tensor_tensor(x[0:T, 0, :], x[0:T, 0, :], x[0:T, 1, :], ALU.add).then_inc(s[sums[2]], 1)
            eng.wait_ge(s[sums[2]], done)
            eng.wait_ge(s["base_ready"], n)
            if not last:
                eng.wait_ge(s["stored"], 16 * n)
            ops.tensor_tensor((out_last if last else out_sb[p])[0:T, :], x[0:T, 0, :], base[p][0:T, :], ALU.add).then_inc(s[sums[3]], 1)

        @block.sync
        def _(sp):
            def load(t, p):
                if isinstance(t, int) and not 0 <= t < NP:
                    return
                if not isinstance(t, int) or t >= 2:
                    sp.wait_ge(s["xln_ready"], t - 1)
                sp.dma_start(x_sb[p][0:T, :], x_pairs[t]).then_inc(x_loaded[p], 16)
                if not isinstance(t, int) or t >= 2:
                    sp.wait_ge(s["xc_turned"], t - 1)
                for b in range(2):
                    sp.dma_start(ctx_sb[p][b * S:(b + 1) * S, :], ctx_pairs[t, b, 0:S, :]).then_inc(ctx_loaded[p], 16)

            def load_residual(t, p):
                if isinstance(t, int) and not 0 <= t < NP:
                    return
                if not isinstance(t, int) or t >= 2:
                    sp.wait_ge(s["x1_ready"], t - 1)
                sp.dma_start(xres[p][0:T, :], x_pairs[t]).then_inc(xres_loaded[p], 16)

            def store(t, p):
                if isinstance(t, int) and not 0 <= t < NP:
                    return
                if isinstance(t, int) and t == NP - 1:
                    sp.wait_ge(s["last_out"], 1)
                    sp.dma_start(out_pairs[t], out_last[0:T, :]).then_inc(s["stored"], 16)
                else:
                    sp.wait_ge(s["out_ready"], t + 1)
                    sp.dma_start(out_pairs[t], out_sb[p][0:T, :]).then_inc(s["stored"], 16)

            sp.dma_start(x_sb[0][0:T, :], x_pairs[0]).then_inc(x_loaded[0], 16)
            sp.dma_start(ctx_sb[0][0:S, :], ctx_pairs[0, 0, 0:S, :]).then_inc(ctx_loaded[0], 16)
            for r in range(2):
                sp.dma_start(wv_sb[:, r, :, :], wv.rearrange("d (c r e) -> d r c e", c=C, r=2)[:, r, :, :]).then_inc(wv_loaded, 16)
            load(1, 1)
            sp.dma_start(gam[:, 0:1], gamma1.rearrange("(d o) -> d o", o=1)).then_inc(w_ffn, 16)
            sp.dma_start(gam[:, 1:2], gamma2.rearrange("(d o) -> d o", o=1)).then_inc(w_ffn, 16)
            sp.dma_start(gates_in[:, 0:1], g_xattn.partition_broadcast(128)).then_inc(w_ffn, 16)
            sp.dma_start(gates_in[:, 1:2], g_ffn.partition_broadcast(128)).then_inc(w_ffn, 16)
            sp.dma_start(wo_sb[:, :, :], wo.rearrange("(c p) f -> p c f", c=C)).then_inc(wo_loaded, 16)
            load_residual(0, 0)
            load(2, 0)
            sp.dma_start(fwq_sb[:, :], fwq).then_inc(w_ffn, 16)
            sp.dma_start(fwdown_sb[:, :], fwdown).then_inc(w_ffn, 16)
            sp.dma_start(fbdown_sb[0:L, :], fbdown.rearrange("(d o) -> d o", o=1)).then_inc(w_ffn, 16)
            sp.dma_start(fwup_in[0:L, :], fwup).then_inc(w_ffn, 16)
            sp.dma_start(fwup_in[L:L + 1, :], fbup.rearrange("(o d) -> o d", o=1)).then_inc(w_ffn, 16)
            sp.dma_start(fbq_sb[:, :], fbq.partition_broadcast(128)).then_inc(w_ffn, 16)
            sp.dma_start(fbo_sb[:, :], fbo.partition_broadcast(128)).then_inc(w_ffn, 16)
            sp.dma_start(fbg_sb[:, :], fbg.partition_broadcast(128)).then_inc(w_ffn, 16)
            sp.dma_start(fwo_sb[:, :], fwo).then_inc(w_ffn, 16)
            sp.dma_start(fwg_sb[:, :], fwg).then_inc(w_ffn, 16)
            sp.dma_start(fwe_sb[:, :, :], fwe.rearrange("e d f -> d e f")).then_inc(w_ffn, 16)

            def step(j, p):
                i = 2 * j + p
                load(i + 6, p)
                load_residual(i + 4, p)
                store(i - 1, 1 - p)

            for i in range(-3, 2):
                step(i // 2, i % 2)
            rounds = (NP - 6) // 2
            with sp.Fori(1, rounds) as j:
                step(j, 0)
                step(j, 1)
            for i in range(2 * rounds, NP + 1):
                step(i // 2, i % 2)
            sp.wait_ge(s["stored"], 16 * (NP + 1))
        N_FFN_LOADS = 15

        @block.gpsimd
        def _(pool):
            nc.gpsimd.memset(minus_half[:, :], -0.5)
            nc.gpsimd.memset(ident[:, :], 0.0).then_inc(consts0, 1)
            pool.wait_ge(consts0, 1)
            nc.gpsimd.affine_select(out=ident[:, :], in_=ident[:, :], compare_op=ALU.not_equal, fill=1.0,
                                    base=0, pattern=[[-1, 128]], channel_multiplier=1).then_inc(consts0, 1)
            nc.gpsimd.memset(hide[:, :], 0.0).then_inc(consts0, 1)

            def make_mask():
                pool.wait_ge(consts0, 3)
                for b in range(2):
                    h = hide[b * G:(b + 1) * G, :]
                    nc.gpsimd.affine_select(out=h, in_=h, compare_op=ALU.is_ge, fill=HIDE, base=0,
                                            pattern=[[-1, S]], channel_multiplier=1).then_inc(consts0, 1)
                    pool.wait_ge(consts0, 4 + b)
                nc.gpsimd.tensor_copy(ident_b[:, :], ident[:, :])
                nc.gpsimd.tensor_copy(hide_b[:, :, :], hide[:, :].unsqueeze(1).to_broadcast([128, C, S])).then_inc(consts, 1)

            def step(j, p):
                i, q = 2 * j + p, 1 - p
                nz, na, nb, nc_, nd = counts(pool, i)
                if isinstance(i, int) and i == -3:
                    make_mask()
                if live(i, 1):
                    pool.wait_ge(s["kv_ready"], nc_)
                    pool.wait_ge(s["fq_ready"], nc_)
                    nc.gpsimd.tensor_tensor(
                        prod1[0:T, 0:HP, :, :],
                        fkv[q][0:T, 0, :].rearrange("p (g d) -> p g d", g=FH).unsqueeze(1).to_broadcast([T, HP, FH, FD]),
                        fq[q][0:T, 0:HP * FD].rearrange("p (h d) -> p h d", h=HP).unsqueeze(2).to_broadcast([T, HP, FH, FD]),
                        ALU.mult).then_inc(s["prod1_pool"], 1)
                if live(i, 4):
                    wait_alone(pool, "moments1", nz)
                    nc.gpsimd.tensor_scalar(ve1[p][0:T, :], mv1[p][0:T, 1:2], LN_EPS, 1.0, ALU.add, ALU.mult).then_inc(s["var1"], 1)
                    pool.wait_ge(s["var1"], nz)
                    nc.gpsimd.tensor_tensor(rstd1[p][0:T, :], ve1[p][0:T, :], minus_half[0:T, 0:1], ALU.pow).then_inc(s["rstd1_ready"], 1)
                if live(i, 0):
                    wait_alone(pool, "ssq_ready", nd)
                    nc.gpsimd.tensor_scalar(ms[p][0:T, :], ssq[p][0:T, :], 1.0 / D, RMS_EPS, ALU.mult, ALU.add).then_inc(s["ms_ready"], 1)
                    pool.wait_ge(s["ms_ready"], nd)
                    nc.gpsimd.tensor_tensor(r2[p][0:T, :], ms[p][0:T, :], minus_half[0:T, 0:1], ALU.pow).then_inc(s["r2_ready"], 1)
                    wait_alone(pool, "r2_ready", nd)
                    nc.gpsimd.tensor_scalar(r2g[p][0:T, :], r2[p][0:T, :], gates[0:T, 1:2], 1.0, ALU.mult, ALU.mult).then_inc(s["r2g_ready"], 1)
                    last = isinstance(i, int) and i == NP - 1
                    if not last and not (isinstance(i, int) and i == 0):
                        outputs(pool, nc.gpsimd, q, nd - 1)
                    wait_alone(pool, "ginv_ready", nd)
                    pool.wait_ge(s["r2g_ready"], nd)
                    nc.gpsimd.tensor_scalar(gate[p][0:T, :], gexp[p][0:T, :], ginv[p][0:T, :], r2g[p][0:T, :], ALU.mult, ALU.mult).then_inc(s["gate_ready"], 1)
                if live(i, 0) and last:
                    outputs(pool, nc.gpsimd, q, nd - 1)
                if live(i, 2):
                    wait_alone(pool, "moments2", nb)
                    nc.gpsimd.tensor_scalar(ve2[p][0:T, 0:1], mv2[p][0:T, 1:2], LN_EPS, 1.0, ALU.add, ALU.mult)
                    nc.gpsimd.tensor_scalar(ve2[p][0:T, 1:2], mv2[p][0:T, 1:2], 1 + RMS_EPS, LN_EPS * RMS_EPS,
                                            ALU.mult, ALU.add).then_inc(s["var2"], 1)
                    pool.wait_ge(s["var2"], nb)
                    nc.gpsimd.tensor_tensor(rstd2[p][0:T, :], ve2[p][0:T, :], minus_half[0:T, :], ALU.pow).then_inc(s["rstd2_ready"], 1)
                if live(i, 3):
                    pool.wait_ge(s["prinv_ready"], na)
                    nc.gpsimd.tensor_tensor(probs[q][0:TG, NC:C, :, 0:S], probs[q][0:TG, NC:C, :, 0:S],
                                            prinv[q][0:TG, NC:C, :].unsqueeze(3).to_broadcast([TG, C - NC, 2, S]),
                                            ALU.mult).then_inc(s["probs_pool"], 1)
                if live(i, 2):
                    wait_alone(pool, "rstd2_ready", nb)
                    nc.gpsimd.tensor_scalar(u_sb[p][0:T, :], x1[p][0:T, :], mv2[p][0:T, 0:1], rstd2[p][0:T, 0:1],
                                            ALU.subtract, ALU.mult).then_inc(s["u_ready"], 1)
                    pool.wait_ge(s["u_ready"], nb)
                    nc.gpsimd.tensor_tensor(ub_sb[p][0:T, :], u_sb[p][0:T, :], fbo_sb[0:T, :], ALU.add).then_inc(s["ub_ready"], 1)

            run(pool, step)

        @block.scalar
        def _(act):
            act.dma_start(ctx_sb[0][S:T, :], ctx_pairs[0, 1, 0:S, :]).then_inc(ctx_loaded[0], 16)
            act.dma_start(wq_sb[:, :, :], wq.rearrange("d (c f) -> d c f", c=C)).then_inc(wq_loaded, 16)
            act.dma_start(wk_sb[:, :, :], wk.rearrange("d (c f) -> d c f", c=C)).then_inc(wk_loaded, 16)
            act.wait_ge(consts0, 1)
            nc.scalar.activation(x2sq[:, 0:1], minus_half[:, 0:1], ACT.Exp)
            act.wait_ge(pads_zeroed, 2)

            def chunks(dst, src, done, n, width, ready):
                for half in range(2):
                    if half < len(done):
                        act.wait_ge(s[done[half]], n)
                    last = nc.scalar.copy(dst[:, half * HC:(half + 1) * HC, :],
                                          src[:, half, 0:HC * width].rearrange("p (c s) -> p c s", c=HC))
                last.then_inc(s[ready], 1)

            def step(j, p):
                i, q = 2 * j + p, 1 - p
                nz, na, nb, nc_, nd = counts(act, i)
                if isinstance(i, int) and i == -2:
                    act.wait_ge(pads_zeroed, 5)
                if live(i, 1):
                    act.wait_ge(s["h_turned"], nc_)
                    nc.scalar.copy(hT[q][:, :], ps_x[:, 0:T]).then_inc(s["hT_ready"], 1)
                if live(i, 3):
                    chunks(qT[q], ps_qkv, ("q_lo", "q_hi"), na, T, "qT_ready")
                if live(i, 1):
                    act.wait_ge(s["c_made"], nc_)
                    nc.scalar.activation(cT[q][0:L, :], ps_kv[0:L, 0:T], ACT.Identity, bias=fbdown_sb[0:L, :]).then_inc(s["cT_ready"], 1)
                if live(i, 2):
                    for half, done in enumerate(("p_lo", "p_hi")):
                        act.wait_ge(s[done], nb)
                        last = nc.scalar.copy(
                            probsT[p][:, half * HC:(half + 1) * HC, :].rearrange("p c (b s) -> p c b s", b=2),
                            ps_pa[:, half, :].rearrange("p (c b s) -> p c b s", c=HC, b=2)[:, :, :, 0:S])
                    last.then_inc(s["probsT_ready"], 1)
                if live(i, 1):
                    act.wait_ge(s["kv_made"], nc_)
                    nc.scalar.copy(fkv[q][0:T, :, :], ps_kv[0:T, 0:2 * D].rearrange("p (n f) -> p n f", n=2)).then_inc(s["kv_ready"], 1)
                if live(i, 0):
                    act.wait_ge(s["o_turned"], nd)
                    nc.scalar.copy(oT[p][:, :], ps_x[:, 0:T]).then_inc(s["oT_ready"], 1)
                if live(i, 3):
                    if isinstance(i, int) and i == -3:
                        act.wait_ge(pads_zeroed, 4)
                    for half, done in enumerate(("k_lo", "k_hi")):
                        act.wait_ge(s[done], na)
                        for r in range(2):
                            last = nc.scalar.copy(
                                kT[q][r * G:(r + 1) * G, half * HC:(half + 1) * HC, :, r, :],
                                k_banks(i)[r * G:(r + 1) * G, half, 0:HC * T].rearrange("p (c b s) -> p c b s", c=HC, b=2))
                    last.then_inc(s["kT_ready"], 1)
                if live(i, 0):
                    act.wait_ge(s["x2_ready"], nd)
                    nc.scalar.activation(x2sq[0:T, :], x2[p][0:T, :], ACT.Square, accum_out=ssq[p][0:T, :]).then_inc(s["ssq_ready"], 1)
                    act.wait_ge(s["x2_turned"], nd)
                    nc.scalar.copy(x2T[p][:, :], ps_x[:, 0:T]).then_inc(s["x2T_ready"], 1)
                if isinstance(i, int) and i == -2:
                    act.wait_ge(w_ffn, 16 * N_FFN_LOADS)
                    nc.scalar.activation(gates[:, :], gates_in[:, :], ACT.Tanh).then_inc(gates_ready, 1)
                if live(i, 2):
                    chunks(attnT[p], ps_pa, ("a_made",), nb, T, "attnT_ready")
                if live(i, 1):
                    act.wait_ge(s["lshift_ready"], nc_)
                    nc.scalar.activation(ps_kv[0:T, 2 * D:4 * D], lshift[q][0:T, :, :].rearrange("p h g -> p (h g)"), ACT.Exp,
                                         scale=float(FD) ** -0.5).then_inc(s["e_ready"], 1)
                if live(i, 3):
                    act.wait_ge(s["v_made"], na)
                    nc.scalar.copy(v_sb[q][:, :, :, :].rearrange("p b c e -> p b (c e)"), ps_qkv[:, :, :]).then_inc(s["v_ready"], 1)
                if live(i, 4):
                    act.wait_ge(s["xc_turned"], nz)
                    nc.scalar.copy(xcT[p][:, :, 0:T], ps_x[:, 0:256].rearrange("p (n s) -> p n s", n=2)[:, :, 0:T]).then_inc(s["xcT_ready"], 1)
                if live(i, 0):
                    act.wait_ge(s["gmax_ready"], nd)
                    nc.scalar.activation(gexp[p][0:T, :], glog[p][0:T, :], ACT.Exp, bias=gmax[p][0:T, :],
                                         accum_out=gsum[p][0:T, :]).then_inc(s["gexp_ready"], 1)
                if live(i, 3):
                    act.wait_ge(s["scores_shifted"], na)
                    nc.scalar.activation(probs[q][0:TG, :, :, 0:S].rearrange("p (n c) r k -> p n (c r) k", n=2),
                                         ps_se[0:TG, :, 0:C * S].rearrange("p n (h k) -> p n h k", h=C), ACT.Exp,
                                         scale=float(DK) ** -0.5).then_inc(s["probs_exp"], 1)
                if live(i, 0):
                    act.wait_ge(s["gate_ready"], nd)
                    for e in range(4 if isinstance(i, int) and i == NP - 1 else E):
                        if e % 4 == 0:
                            act.wait_ge(s["experts_made"], nd + nd - 1 + e // 4)
                        last = nc.scalar.activation(expert[p][0:T, e, :], ps_pa[0:T, e // 4, (e % 4) * D:(e % 4 + 1) * D],
                                                    ACT.Copy, scale=gate[p][0:T, e:e + 1])
                    last.then_inc(s["experts_ready"], 1)

            run(act, step)

        @block.vector
        def _(dve):
            for p in range(2):
                nc.vector.memset(xcT[p][:, :, :], 0.0).then_inc(pads_zeroed, 1)
            for p in range(2):
                ins = nc.vector.memset(cT[p][L:L + 1, :], 1.0)
            ins.then_inc(s["stored"], 16)

            def scale_weights():
                dve.wait_ge(w_ffn, 16 * N_FFN_LOADS)
                nc.vector.tensor_scalar(fwq_sb[:, :], fwq_sb[:, :], gam[:, 0:1], None, ALU.mult)
                nc.vector.tensor_scalar(fwdown_sb[:, :], fwdown_sb[:, :], gam[:, 0:1], None, ALU.mult)
                nc.vector.tensor_scalar(fwg_sb[:, :], fwg_sb[:, :], gam[:, 1:2], None, ALU.mult)
                nc.vector.tensor_scalar(fwe_sb[:, :, :], fwe_sb[:, :, :], gam[:, 1:2], None, ALU.mult)
                up = fwup_in[0:L + 1, :].rearrange("p (h n d) -> p h n d", h=FH, n=2)
                nc.vector.tensor_copy(fwup_sb[0:L + 1, 0, :].rearrange("p (h d) -> p h d", h=FH), up[:, :, 0, :])
                nc.vector.tensor_copy(fwup_sb[0:L + 1, 1, :].rearrange("p (d h) -> p h d", h=FH), up[:, :, 1, :]).then_inc(scaled, 1)

            def step(j, p):
                i, q = 2 * j + p, 1 - p
                nz, na, nb, nc_, nd = counts(dve, i)
                if isinstance(i, int) and i == -3:
                    nc.vector.memset(kT[0][:, :, :, :, :], 0.0).then_inc(pads_zeroed, 1)
                    nc.vector.memset(probs[0][:, :, :, :], 0.0).then_inc(pads_zeroed, 1)
                if isinstance(i, int) and i == -2:
                    scale_weights()
                if live(i, 0):
                    dve.wait_ge(s["prod2_ready"], nd)
                    nc.vector.tensor_reduce(oraw[p][0:T, :, :], prod2[0:T, :, :, :], AX.X, ALU.add).then_inc(s["oraw_ready"], 1)
                    dve.wait_ge(s["oraw_ready"], nd)
                    dve.wait_ge(s["einv_ready"], nd)
                    nc.vector.tensor_tensor(onorm[p][0:T, :].rearrange("p (h d) -> p h d", h=FH), oraw[p][0:T, :, :],
                                            einv[p][0:T, :].unsqueeze(2).to_broadcast([T, FH, FD]), ALU.mult).then_inc(s["onorm_ready"], 1)
                if live(i, 1):
                    dve.wait_ge(s["fq_made"], nc_)
                    nc.vector.tensor_tensor(fq[q][0:T, :], ps_x[0:T, 0:D], fbq_sb[0:T, :], ALU.add).then_inc(s["fq_ready"], 1)
                    dve.wait_ge(s["kv_ready"], nc_)
                    dve.wait_ge(s["fq_ready"], nc_)
                    nc.vector.tensor_tensor(
                        prod1[0:T, HP:FH, :, :],
                        ps_kv[0:T, 0:D].rearrange("p (g d) -> p g d", g=FH).unsqueeze(1).to_broadcast([T, FH - HP, FH, FD]),
                        fq[q][0:T, HP * FD:D].rearrange("p (h d) -> p h d", h=FH - HP).unsqueeze(2).to_broadcast([T, FH - HP, FH, FD]),
                        ALU.mult).then_inc(s["prod1_ready"], 1)
                if live(i, 4):
                    dve.wait_ge(x_loaded[p], 16 * (j + 3))
                    nc.vector.bn_stats(st1[p][0:T, :], x_sb[p][0:T, :]).then_inc(s["stats1"], 1)
                if live(i, 0):
                    dve.wait_ge(s["o_made"], nd)
                    dve.wait_ge(s["ub_ready"], nd)
                    nc.vector.tensor_tensor(x2[p][0:T, :], ps_x[0:T, 0:D], ub_sb[p][0:T, :], ALU.add).then_inc(s["x2_ready"], 1)
                if live(i, 4):
                    wait_alone(dve, "stats1", nz)
                    nc.vector.bn_aggr(mv1[p][0:T, :], st1[p][0:T, :]).then_inc(s["moments1"], 1)
                if live(i, 1):
                    dve.wait_ge(s["prod1_pool"], nc_)
                    dve.wait_ge(s["prod1_ready"], nc_)
                    nc.vector.tensor_reduce(logit[q][0:T, :, :], prod1[0:T, :, :, :], AX.X, ALU.add).then_inc(s["logit_ready"], 1)
                if live(i, 4):
                    dve.wait_ge(s["rstd1_ready"], nz)
                    nc.vector.tensor_scalar(xln[p][0:T, :], x_sb[p][0:T, :], mv1[p][0:T, 0:1], rstd1[p][0:T, :],
                                            ALU.subtract, ALU.mult).then_inc(s["xln_ready"], 1)
                if live(i, 1):
                    dve.wait_ge(s["logit_ready"], nc_)
                    nc.vector.tensor_reduce(lmax[q][0:T, :], logit[q][0:T, :, :], AX.X, ALU.max).then_inc(s["lmax_ready"], 1)
                if live(i, 0):
                    dve.wait_ge(s["glog_made"], nd)
                    dve.wait_ge(s["r2_ready"], nd)
                    nc.vector.scalar_tensor_tensor(out=glog[p][0:T, :], in0=ps_x[0:T, 256:256 + E], scalar=r2[p][0:T, :],
                                                   in1=fbg_sb[0:T, :], op0=ALU.mult, op1=ALU.add).then_inc(s["glog_ready"], 1)
                if live(i, 1):
                    dve.wait_ge(s["lmax_ready"], nc_)
                    nc.vector.tensor_tensor(lshift[q][0:T, :, :], logit[q][0:T, :, :],
                                            lmax[q][0:T, :].unsqueeze(2).to_broadcast([T, FH, FH]),
                                            ALU.subtract).then_inc(s["lshift_ready"], 1)
                if live(i, 0):
                    dve.wait_ge(s["x2_ready"], nd)
                    nc.vector.scalar_tensor_tensor(out=base[p][0:T, :], in0=x2[p][0:T, :], scalar=gates[0:T, 1:2],
                                                   in1=x1[p][0:T, :], op0=ALU.mult, op1=ALU.add).then_inc(s["base_ready"], 1)
                if live(i, 0):
                    dve.wait_ge(s["glog_ready"], nd)
                    nc.vector.tensor_reduce(gmax[p][0:T, :], glog[p][0:T, :], AX.X, ALU.max, negate=True).then_inc(s["gmax_ready"], 1)
                if live(i, 1):
                    dve.wait_ge(s["e_ready"], nc_)
                    nc.vector.tensor_reduce(esum[q][0:T, :], ps_kv[0:T, 2 * D:4 * D].rearrange("p (h g) -> p h g", h=FH),
                                            AX.X, ALU.add).then_inc(s["esum_ready"], 1)
                    nc.vector.tensor_tensor(
                        prod2[0:T, :, :, :],
                        ps_kv[0:T, 2 * D:4 * D].rearrange("p (h g) -> p h g", h=FH).unsqueeze(2).to_broadcast([T, FH, FD, FH]),
                        fkv[q][0:T, 1, :].rearrange("p (d g) -> p d g", d=FD).unsqueeze(1).to_broadcast([T, FH, FD, FH]),
                        ALU.mult).then_inc(s["prod2_ready"], 1)
                    dve.wait_ge(s["esum_ready"], nc_)
                    nc.vector.reciprocal(einv[q][0:T, :], esum[q][0:T, :]).then_inc(s["einv_ready"], 1)
                if isinstance(i, int) and i == -3:
                    nc.vector.memset(kT[1][:, :, :, :, :], 0.0)
                    nc.vector.memset(probs[1][:, :, :, :], 0.0).then_inc(pads_zeroed, 1)
                if live(i, 3):
                    dve.wait_ge(s["scores_made"], na)
                    nc.vector.tensor_reduce(nmax[q][0:TG, :, :], ps_se[0:TG, :, 0:C * S].rearrange("p n (h k) -> p n h k", h=C),
                                            AX.X, ALU.max, negate=True).then_inc(s["nmax_ready"], 1)
                if live(i, 0):
                    dve.wait_ge(s["gexp_ready"], nd)
                    nc.vector.reciprocal(ginv[p][0:T, :], gsum[p][0:T, :]).then_inc(s["ginv_ready"], 1)
                if isinstance(i, int) and i == -2:
                    dve.wait_ge(gates_ready, 1)
                if live(i, 2):
                    dve.wait_ge(s["y_made"], nb)
                    dve.wait_ge(xres_loaded[p], 16 * (j + 2))
                    nc.vector.scalar_tensor_tensor(out=x1[p][0:T, :], in0=ps_x[0:T, 0:D], scalar=gates[0:T, 0:1],
                                                   in1=xres[p][0:T, :], op0=ALU.mult, op1=ALU.add).then_inc(s["x1_ready"], 1)
                    dve.wait_ge(s["x1_ready"], nb)
                    nc.vector.bn_stats(st2[p][0:T, :], x1[p][0:T, :]).then_inc(s["stats2"], 1)
                    wait_alone(dve, "stats2", nb)
                    nc.vector.bn_aggr(mv2[p][0:T, :], st2[p][0:T, :]).then_inc(s["moments2"], 1)
                if live(i, 3):
                    dve.wait_ge(s["probs_exp"], na)
                    nc.vector.tensor_reduce(psums[q][0:TG, :, :], probs[q][0:TG, :, :, 0:S], AX.X, ALU.add).then_inc(s["psum_ready"], 1)
                if live(i, 2):
                    dve.wait_ge(s["rstd2_ready"], nb)
                    nc.vector.tensor_scalar(h_sb[p][0:T, :], x1[p][0:T, :], mv2[p][0:T, 0:1], rstd2[p][0:T, 1:2],
                                            ALU.subtract, ALU.mult).then_inc(s["h_ready"], 1)
                if live(i, 3):
                    dve.wait_ge(s["psum_ready"], na)
                    nc.vector.reciprocal(prinv[q][0:TG, :, :], psums[q][0:TG, :, :]).then_inc(s["prinv_ready"], 1)
                    dve.wait_ge(s["prinv_ready"], na)
                    nc.vector.tensor_tensor(probs[q][0:TG, 0:NC, :, 0:S], probs[q][0:TG, 0:NC, :, 0:S],
                                            prinv[q][0:TG, 0:NC, :].unsqueeze(3).to_broadcast([TG, NC, 2, S]),
                                            ALU.mult).then_inc(s["probs_ready"], 1)

            run(dve, step)
            dve.wait_ge(s["experts_made"], 2 * NP)
            dve.wait_ge(s["gate_ready"], NP)
            last_p = (NP - 1) % 2
            nc.vector.tensor_tensor(expert[last_p][0:T, 4:8, :], ps_pa[0:T, 1, :].rearrange("p (e f) -> p e f", e=4),
                                    gate[last_p][0:T, 4:8].unsqueeze(2).to_broadcast([T, 4, D]), ALU.mult).then_inc(s["last_half"], 1)
            dve.wait_ge(s["last_half"], 1)
            outputs(dve, nc.vector, last_p, NP, last=True)

        @block.tensor
        def _(pe):
            pe.wait_ge(consts0, 2)

            def warm_up(n):
                for _n in range(n):
                    nc.tensor.matmul(ps_se[:, 0, 0:128], ident[:, :], ident[:, :], start=True, stop=True)

            warm_up(WARM_UP)

            def mm(o, lhsT, rhs, start=True, stop=True):
                return nc.tensor.matmul(o, lhsT, rhs, start=start, stop=stop, skip_group_check=True)

            def project(dst, w, rhs, half, done):
                for ch in range(half * HC, (half + 1) * HC):
                    ins = mm(dst[:, half, ch % HC * T:(ch % HC + 1) * T], w[:, ch, :], rhs)
                ins.then_inc(s[done], 1)

            def turn_probs(i, p, nb, nc_, nd):
                pe.wait_ge(s["probs_ready"], nb)
                pe.wait_ge(s["probs_pool"], nb)
                if live(i, -1) and not (isinstance(i, int) and i < 1):
                    pe.wait_ge(s["experts_ready"], nd - 1)
                elif live(i, 1):
                    pe.wait_ge(s["attnT_ready"], nc_)
                for ch in range(C):
                    ins = nc.tensor.transpose(ps_pa[:, ch // HC, ch % HC * 128:ch % HC * 128 + TG],
                                              probs[p][0:TG, ch, :, :].rearrange("p r k -> p (r k)"), ident[0:TG, 0:TG])
                    if ch % HC == HC - 1:
                        ins.then_inc(s["p_hi" if ch // HC else "p_lo"], 1)

            def turn_h(q, nc_):
                pe.wait_ge(s["h_ready"], nc_)
                nc.tensor.transpose(ps_x[:, 0:T], h_sb[q][0:T, :], ident[0:T, 0:T]).then_inc(s["h_turned"], 1)

            def keep_up(i, n):
                if isinstance(i, int) and i + 3 >= NP:
                    for _n in range(n):
                        nc.tensor.matmul(ps_qkv[:, 0, 0:256], ident[:, :], ident[:, :].unsqueeze(1).to_broadcast([128, 2, 128]),
                                         start=True, stop=True)

            def step(j, p):
                i, q = 2 * j + p, 1 - p
                nz, na, nb, nc_, nd = counts(pe, i)
                if isinstance(i, int) and i == -3:
                    warm_up(2)
                    pe.wait_ge(wq_loaded, 16)
                if isinstance(i, int) and i == -1:
                    pe.wait_ge(scaled, 1)
                if live(i, 3):
                    pe.wait_ge(s["xcT_ready"], na)
                    if live(i, 2):
                        pe.wait_ge(s["v_ready"], nb)
                    project(ps_qkv, wq_sb, xcT[q][:, 0, 0:T], 0, "q_lo")
                if isinstance(i, int) and i + 3 == NP:
                    pe.wait_ge(s["v_ready"], NP)
                if isinstance(i, int) and i + 3 >= NP:
                    keep_up(i, (1, 4, 13)[i + 3 - NP])
                full = not (isinstance(i, int) and i < 1)
                if live(i, 1) and full:
                    turn_h(q, nc_)
                if live(i, 3):
                    project(ps_qkv, wq_sb, xcT[q][:, 0, 0:T], 1, "q_hi")
                if live(i, 1) and not full:
                    turn_h(q, nc_)
                if live(i, 1):
                    keep_up(i, 1)
                    pe.wait_ge(s["hT_ready"], nc_)
                    mm(ps_x[0:T, 0:D], hT[q][:, :], fwq_sb[:, :]).then_inc(s["fq_made"], 1)
                    if live(i, 0):
                        pe.wait_ge(s["prod2_ready"], nd)
                    mm(ps_kv[0:L, 0:T], fwdown_sb[:, :], hT[q][:, :]).then_inc(s["c_made"], 1)
                late = isinstance(i, int) and i == -2
                if live(i, 2) and not late:
                    turn_probs(i, p, nb, nc_, nd)
                if live(i, 1):
                    pe.wait_ge(s["cT_ready"], nc_)
                    mm(ps_kv[0:T, 0:2 * D], cT[q][0:L + 1, :], fwup_sb[0:L + 1, :, :].rearrange("p n f -> p (n f)")).then_inc(s["kv_made"], 1)
                if live(i, 3):
                    if isinstance(i, int) and i == -3:
                        pe.wait_ge(wk_loaded, 16)
                    else:
                        pe.wait_ge(s["qT_ready"], na)
                    project(k_banks(i), wk_sb, xcT[q][:, 1, 0:T], 0, "k_lo")
                if live(i, 0):
                    keep_up(i, 1)
                    pe.wait_ge(s["onorm_ready"], nd)
                    if live(i, 1):
                        pe.wait_ge(s["fq_ready"], nc_)
                    else:
                        pe.wait_ge(s["glog_ready"], nd - 1)
                    nc.tensor.transpose(ps_x[:, 0:T], onorm[p][0:T, :], ident[0:T, 0:T]).then_inc(s["o_turned"], 1)
                if live(i, 3):
                    project(k_banks(i), wk_sb, xcT[q][:, 1, 0:T], 1, "k_hi")
                if live(i, 2) and late:
                    turn_probs(i, p, nb, nc_, nd)
                if live(i, 0):
                    keep_up(i, 1)
                    pe.wait_ge(s["oT_ready"], nd)
                    mm(ps_x[0:T, 0:D], oT[p][:, :], fwo_sb[:, :]).then_inc(s["o_made"], 1)
                for k in range(C):
                    if live(i, 2):
                        if k == 0:
                            wait_alone(pe, "probsT_ready", nb)
                        for r in range(2):
                            ch = (k + r * HC) % C
                            for bt in range(2):
                                ins = mm(ps_pa[r * G:r * G + DK, ch // HC, ch % HC * T + bt * S:ch % HC * T + (bt + 1) * S],
                                         v_sb[p][r * G:r * G + S, bt, ch, :], probsT[p][r * G:r * G + S, ch, bt * S:(bt + 1) * S])
                        if k == C - 1:
                            ins.then_inc(s["a_made"], 1)
                    if live(i, 0) and k == HC - 1:
                        if not live(i, 2):
                            keep_up(i, 1)
                        pe.wait_ge(s["x2_ready"], nd)
                        nc.tensor.transpose(ps_x[:, 0:T], x2[p][0:T, :], ident[0:T, 0:T]).then_inc(s["x2_turned"], 1)
                if live(i, 0):
                    if not live(i, 2):
                        keep_up(i, 1)
                    pe.wait_ge(s["x2T_ready"], nd)
                    mm(ps_x[0:T, 256:256 + E], x2T[p][:, :], fwg_sb[:, :]).then_inc(s["glog_made"], 1)
                if live(i, 3):
                    if isinstance(i, int) and i == -3:
                        pe.wait_ge(wv_loaded, 32)
                        pe.wait_ge(s["qT_ready"], na)
                    else:
                        pe.wait_ge(s["kT_ready"], na)
                    for bt in range(2):
                        for r in range(2):
                            ins = mm(ps_qkv[r * G:(r + 1) * G, bt, :], xcT[q][:, 1, bt * S:bt * S + G],
                                     wv_sb[:, r, :, :].rearrange("p c e -> p (c e)"))
                    ins.then_inc(s["v_made"], 1)
                if live(i, 4):
                    pe.wait_ge(s["xln_ready"], nz)
                    pe.wait_ge(ctx_loaded[p], 32 * (j + 3))
                    if live(i, 0):
                        pe.wait_ge(s["glog_ready"], nd)
                    elif live(i, 1):
                        pe.wait_ge(s["fq_ready"], nc_)
                    elif i > -4:
                        pe.wait_ge(s["xcT_ready"], nz - 1)
                    nc.tensor.transpose(ps_x[:, 0:T], xln[p][0:T, :], ident[0:T, 0:T])
                    nc.tensor.transpose(ps_x[:, 128:128 + T], ctx_sb[p][0:T, :], ident[0:T, 0:T]).then_inc(s["xc_turned"], 1)
                if live(i, 3):
                    if isinstance(i, int) and i == -3:
                        pe.wait_ge(consts, 1)
                        pe.wait_ge(s["kT_ready"], na)
                    for half in range(2):
                        mm(ps_se[0:TG, half, 0:C * S], ident_b[0:TG, 0:TG], hide_b[0:TG, :, :].rearrange("p c k -> p (c k)"), stop=False)
                    for ch in range(C):
                        for bt in range(2):
                            ins = mm(ps_se[bt * G:bt * G + S, ch // HC, ch % HC * T:(ch % HC + 1) * T],
                                     qT[q][:, ch, bt * S:(bt + 1) * S],
                                     kT[q][:, ch, bt, :, :].rearrange("p r k -> p (r k)"), start=False, stop=False)
                    ins.then_inc(s["scores_made"], 1)
                if live(i, 2):
                    keep_up(i, 2)
                    if isinstance(i, int) and i == -2:
                        pe.wait_ge(wo_loaded, 16)
                    pe.wait_ge(s["attnT_ready"], nb)
                    if live(i, 4):
                        pe.wait_ge(s["xcT_ready"], nz)
                    elif live(i, 0):
                        pe.wait_ge(s["glog_ready"], nd)
                    for ch in range(C):
                        ins = mm(ps_x[0:T, 0:D], attnT[p][:, ch, :], wo_sb[:, ch, :], start=(ch == 0), stop=(ch == C - 1))
                    ins.then_inc(s["y_made"], 1)
                if live(i, 3):
                    pe.wait_ge(s["nmax_ready"], na)
                    for half in range(2):
                        ins = mm(ps_se[0:TG, half, 0:C * S], ident_b[0:TG, 0:TG],
                                 nmax[q][0:TG, half, :].unsqueeze(2).to_broadcast([TG, C, S]), start=False)
                    ins.then_inc(s["scores_shifted"], 1)
                if live(i, 0):
                    if not live(i, 2):
                        pe.wait_ge(s["experts_ready"], nd - 1)
                    for n in range(2):
                        mm(ps_pa[0:T, n, :], x2T[p][:, :],
                           fwe_sb[:, n * 4:(n + 1) * 4, :].rearrange("p e f -> p (e f)")).then_inc(s["experts_made"], 1)

            run(pe, step)


_INS = ["x", "ctx_1024", "g_xattn", "g_ffn", "L0_xattn_Wq", "L0_xattn_Wk", "L0_xattn_Wv", "L0_xattn_Wo",
        "L0_ffn_gamma1", "L0_ffn_Wq", "L0_ffn_bq", "L0_ffn_Wdown", "L0_ffn_bdown", "L0_ffn_Wup", "L0_ffn_bup",
        "L0_ffn_Wo", "L0_ffn_bo", "L0_ffn_gamma2", "L0_ffn_Wg", "L0_ffn_bg", "L0_ffn_We"]


def kernel(**inputs):
    import concourse.bacc as bacc
    from concourse.bass_utils import run_bass_kernel_spmd

    nc = bacc.Bacc("TRN2", target_bir_lowering=False, num_devices=1)
    arrays, args = {}, []
    for name in _INS:
        a = np.ascontiguousarray(inputs[name])
        arrays[f"in_{name}"] = a
        args.append(nc.dram_tensor(f"in_{name}", a.shape, mybir.dt.from_np(a.dtype), kind="ExternalInput").ap())
    out = nc.dram_tensor("out", inputs["x"].shape, F32, kind="ExternalOutput").ap()
    build(nc, *args, out)
    r = run_bass_kernel_spmd(nc, [arrays], core_ids=[0])
    return r.results[0]["out"]
```
